# Optimizing a Trainium2 kernel written in Bass

```python
import numpy as np
import jax
import jax.numpy as jnp

def _softmax(x, axis=-1):
    return jax.nn.softmax(x, axis=axis)

def _gelu(x):
    return jax.nn.gelu(x, approximate=True)

def _silu(x):
    return jax.nn.silu(x)

def _sigmoid(x):
    return jax.nn.sigmoid(x)

def _layernorm(x, axis=-1, eps=1e-05):
    m = jnp.mean(x, axis=axis, keepdims=True)
    v = jnp.var(x, axis=axis, keepdims=True)
    return (x - m) / jnp.sqrt(v + eps)

def _scatter_add(tgt, idx, src, axis=0):
    return tgt.at[idx].add(src)

def _segment_sum(src, seg, n):
    return jax.ops.segment_sum(src, seg, n)
kernel_name = 'mk_macaron_d1_jaxref_r8_1e7ba0'

def setup_inputs(seed: int=0):
    np.random.seed(seed)
    _w = jnp.asarray

    def _L0_attn_setup():
        import jax, jax.numpy as jnp
        import numpy as np
        import math
        B, S, E = (2, 256, 128)
        H, DK, DV = (16, 64, 64)

        def _rope(q, k):
            D = q.shape[-1]
            theta = 10000.0 ** (jnp.arange(0, D, 2, dtype=jnp.float32) / D)
            pos = jnp.arange(q.shape[-2], dtype=jnp.float32)
            freqs = pos[:, None] * (1.0 / theta)[None, :]
            emb = jnp.concatenate([freqs, freqs], axis=-1)
            cos = jnp.cos(emb)[None, None]
            sin = jnp.sin(emb)[None, None]

            def rotate(x):
                x1 = x[..., ::2]
                x2 = x[..., 1::2]
                return jnp.stack([-x2, x1], axis=-1).reshape(x.shape)
            return (q * cos + rotate(q) * sin, k * cos + rotate(k) * sin)
        key = jax.random.key(seed)
        ks = jax.random.split(key, 9)
        sE = 1.0 / math.sqrt(E)
        sV = 1.0 / math.sqrt(H * DV)
        return {'x': jax.random.normal(ks[0], (B, S, E), dtype=jnp.float32), 'wq': jax.random.uniform(ks[1], (H * DK, E), jnp.float32, -sE, sE), 'bq': jax.random.uniform(ks[2], (H * DK,), jnp.float32, -sE, sE), 'wk': jax.random.uniform(ks[3], (H * DK, E), jnp.float32, -sE, sE), 'bk': jax.random.uniform(ks[4], (H * DK,), jnp.float32, -sE, sE), 'wv': jax.random.uniform(ks[5], (H * DV, E), jnp.float32, -sE, sE), 'bv': jax.random.uniform(ks[6], (H * DV,), jnp.float32, -sE, sE), 'wo': jax.random.uniform(ks[7], (E, H * DV), jnp.float32, -sV, sV), 'bo': jax.random.uniform(ks[8], (E,), jnp.float32, -sV, sV)}
    _L0_attn_in = _L0_attn_setup()

    def _L0_ffn_setup():
        import jax, jax.numpy as jnp
        import numpy as np
        DIM = 128

        def _reference_tuple_inner(x, W_r, W_k, W_v, mu_r, mu_k):
            B, T, C = x.shape
            x_prev = jnp.concatenate([jnp.zeros((B, 1, C), x.dtype), x[:, :-1, :]], axis=1)
            xr = mu_r * x + (1.0 - mu_r) * x_prev
            xk = mu_k * x + (1.0 - mu_k) * x_prev
            r = jax.nn.sigmoid(jnp.einsum('btc,dc->btd', xr, W_r))
            k = jnp.einsum('btc,dc->btd', xk, W_k)
            k_act = jnp.square(jax.nn.relu(k))
            out = r * jnp.einsum('btc,dc->btd', k_act, W_v)
            new_state = x[:, -1, :]
            return (out, new_state)
        key = jax.random.key(seed)
        ks = jax.random.split(key, 6)
        B, T, C = (8, 256, DIM)
        x = jax.random.normal(ks[0], (B, T, C), dtype=jnp.float32)
        s = 1.0 / np.sqrt(C)
        W_r = jax.random.uniform(ks[1], (C, C), jnp.float32, -s, s)
        W_k = jax.random.uniform(ks[2], (C, C), jnp.float32, -s, s)
        W_v = jax.random.uniform(ks[3], (C, C), jnp.float32, -s, s)
        mu_r = jax.random.uniform(ks[4], (C,), jnp.float32)
        mu_k = jax.random.uniform(ks[5], (C,), jnp.float32)
        return {'x': x, 'W_r': W_r, 'W_k': W_k, 'W_v': W_v, 'mu_r': mu_r, 'mu_k': mu_k}
    _L0_ffn_in = _L0_ffn_setup()
    _d = {'L0_attn_x': _L0_attn_in['x'], 'L0_attn_wq': _L0_attn_in['wq'], 'L0_attn_bq': _L0_attn_in['bq'], 'L0_attn_wk': _L0_attn_in['wk'], 'L0_attn_bk': _L0_attn_in['bk'], 'L0_attn_wv': _L0_attn_in['wv'], 'L0_attn_bv': _L0_attn_in['bv'], 'L0_attn_wo': _L0_attn_in['wo'], 'L0_attn_bo': _L0_attn_in['bo'], 'L0_ffn_W_r': _L0_ffn_in['W_r'], 'L0_ffn_W_k': _L0_ffn_in['W_k'], 'L0_ffn_W_v': _L0_ffn_in['W_v'], 'L0_ffn_mu_r': _L0_ffn_in['mu_r'], 'L0_ffn_mu_k': _L0_ffn_in['mu_k']}
    _x0 = _d['L0_attn_x']
    _d['L0_attn_x'] = jax.random.normal(jax.random.fold_in(jax.random.key(seed), 1), (2, 1024, 128), dtype=_x0.dtype)
    del _x0
    return _d

def reference(L0_attn_x, L0_attn_wq, L0_attn_bq, L0_attn_wk, L0_attn_bk, L0_attn_wv, L0_attn_bv, L0_attn_wo, L0_attn_bo, L0_ffn_W_r, L0_ffn_W_k, L0_ffn_W_v, L0_ffn_mu_r, L0_ffn_mu_k):

    def _L0_attn_ref(x, wq, bq, wk, bk, wv, bv, wo, bo):
        import jax, jax.numpy as jnp
        import numpy as np
        import math
        B, S, E = (2, 256, 128)
        H, DK, DV = (16, 64, 64)

        def _rope(q, k):
            D = q.shape[-1]
            theta = 10000.0 ** (jnp.arange(0, D, 2, dtype=jnp.float32) / D)
            pos = jnp.arange(q.shape[-2], dtype=jnp.float32)
            freqs = pos[:, None] * (1.0 / theta)[None, :]
            emb = jnp.concatenate([freqs, freqs], axis=-1)
            cos = jnp.cos(emb)[None, None]
            sin = jnp.sin(emb)[None, None]

            def rotate(x):
                x1 = x[..., ::2]
                x2 = x[..., 1::2]
                return jnp.stack([-x2, x1], axis=-1).reshape(x.shape)
            return (q * cos + rotate(q) * sin, k * cos + rotate(k) * sin)
        Bx, Sx, Ex = x.shape
        q = (x @ wq.T + bq).reshape(Bx, Sx, H, DK).transpose(0, 2, 1, 3)
        k = (x @ wk.T + bk).reshape(Bx, Sx, H, DK).transpose(0, 2, 1, 3)
        v = (x @ wv.T + bv).reshape(Bx, Sx, H, DV).transpose(0, 2, 1, 3)
        q, k = _rope(q, k)
        scores = jnp.einsum('bhqd,bhkd->bhqk', q, k)
        causal = jnp.triu(jnp.ones((Sx, Sx), dtype=bool), k=1)
        scores = jnp.where(causal[None, None], -jnp.inf, scores)
        attn = jax.nn.softmax(scores / math.sqrt(DK), axis=-1)
        out = jnp.einsum('bhqk,bhkd->bhqd', attn, v)
        out = out.transpose(0, 2, 1, 3).reshape(Bx, Sx, H * DV)
        return out @ wo.T + bo

    def _L0_ffn_ref(x, W_r, W_k, W_v, mu_r, mu_k):
        import jax, jax.numpy as jnp
        import numpy as np
        DIM = 128

        def _reference_tuple_inner(x, W_r, W_k, W_v, mu_r, mu_k):
            B, T, C = x.shape
            x_prev = jnp.concatenate([jnp.zeros((B, 1, C), x.dtype), x[:, :-1, :]], axis=1)
            xr = mu_r * x + (1.0 - mu_r) * x_prev
            xk = mu_k * x + (1.0 - mu_k) * x_prev
            r = jax.nn.sigmoid(jnp.einsum('btc,dc->btd', xr, W_r))
            k = jnp.einsum('btc,dc->btd', xk, W_k)
            k_act = jnp.square(jax.nn.relu(k))
            out = r * jnp.einsum('btc,dc->btd', k_act, W_v)
            new_state = x[:, -1, :]
            return (out, new_state)
        return _reference_tuple_inner(x, W_r, W_k, W_v, mu_r, mu_k)[0]
    x = L0_attn_x
    x = x + 0.5 * _L0_ffn_ref(_layernorm(x, axis=-1), L0_ffn_W_r, L0_ffn_W_k, L0_ffn_W_v, L0_ffn_mu_r, L0_ffn_mu_k)
    x = x + _L0_attn_ref(_layernorm(x, axis=-1), L0_attn_wq, L0_attn_bq, L0_attn_wk, L0_attn_bk, L0_attn_wv, L0_attn_bv, L0_attn_wo, L0_attn_bo)
    x = x + 0.5 * _L0_ffn_ref(_layernorm(x, axis=-1), L0_ffn_W_r, L0_ffn_W_k, L0_ffn_W_v, L0_ffn_mu_r, L0_ffn_mu_k)
    return x

_drawn_inputs = setup_inputs


def setup_inputs(seed=0):
    import zlib

    import numpy as np

    out = dict(_drawn_inputs(seed))
    spreads = {}
    factors = {'L0_attn_wq': 4.98,
     'L0_attn_bq': 8.0,
     'L0_attn_wk': 4.941,
     'L0_attn_bk': 8.0,
     'L0_attn_bo': 2.983,
     'L0_ffn_W_r': 3.139,
     'L0_ffn_mu_r': 6.191}
    for name, (base, spread) in spreads.items():
        noise = np.random.default_rng([zlib.crc32(name.encode()), seed]).standard_normal(out[name].shape)
        drawn = base * np.exp(spread * noise) if base else spread * noise
        out[name] = jnp.asarray(drawn.astype(out[name].dtype))
    for name, factor in factors.items():
        out[name] = (out[name] * factor).astype(out[name].dtype)
    return out
```

```python
from contextlib import ExitStack

import numpy as np

import concourse.bass as bass
from concourse import mybir

ALU = mybir.AluOpType
ACT = mybir.ActivationFunctionType
F32 = mybir.dt.float32
F32R = mybir.dt.float32r
BF16 = mybir.dt.bfloat16
AX_X = mybir.AxisListType.X

P = 128
B, S, E = 2, 1024, 128
H, DK = 16, 64
TILES = B * S // P
CHUNK = 512
CHUNKS = B * S // CHUNK
PER_CHUNK = CHUNK // P
QUAD = 4
QUADS = H // QUAD
ITERS = B * QUADS
HALF = DK // 2
EPS = 1e-5
SCALE = 1.0 / 8.0
MASKED = -1e30

W_QK = 4 * P
W_V = QUAD * DK
W_ALL = W_QK + W_V

UNITS = 2 * QUAD
BLOCKS = [4, 8]
BLOCK0 = [sum(BLOCKS[v % 2] for v in range(u)) for u in range(UNITS + 1)]
ALL_BLOCKS = BLOCK0[UNITS]
TILE_LEN = [(t + 1) * P for t in range(8)]
P_OFF = [sum(TILE_LEN[4 * g + k] for k in range(4) if 4 * g + k < t) + (0 if g == 0 else sum(TILE_LEN[:4]))
         for t in range(8) for g in [t // 4]]
P_COLS = sum(TILE_LEN)

PROJ = 16
FILLS = PROJ + 2
PROJ_ORDER = [(0, 0), (0, 1), (0, 4), (0, 5), (0, 2), (0, 3), (0, 6), (0, 7),
              (1, 0), (1, 1), (1, 4), (1, 5), (1, 2), (1, 3), (1, 6), (1, 7)]
PROJ_AT = [(1, 1), (1, 4), (2, 0), (2, 1), (2, 2), (2, 3), (3, 1), (3, 4),
           (4, 0), (4, 1), (4, 2), (4, 3), (5, 0), (5, 2), (5, 4), (5, 6)]
OUT_AT = [(7, 4), (0, 1)]
SCORE_AT = [[0, 1, 2, 3], [0, 1, 2, 3]]
CONSUME, ROUND = 1, 3


def first_col(g, j):
    return max(0, j - 4 * g) * P


def at(i, ahead, per, rest):
    return i * per + (ahead * per + rest)


def schedule(units, last):
    steps = []
    for n, u in enumerate(units):
        ahead = 1 if n and u == 0 else 0
        nxt = (ahead + 1, 0) if u == UNITS - 1 else (ahead, u + 1)
        before = SCORE_AT[(u - 1) % 2]
        for j in range(BLOCKS[u % 2]):
            now = SCORE_AT[u % 2]
            ready = [(*nxt, k) for k in range(4) if now[k] == j - 1]
            if j == 0:
                ready = [(ahead, u, k) for k in range(4) if before[k] == BLOCKS[(u - 1) % 2] - 1]
            steps.append(dict(
                ahead=ahead, unit=u, j=j,
                score=(*nxt, now.index(j)) if j in now else None, ready=ready,
                fills=[] if last else [f for f, place in enumerate(PROJ_AT) if place == (u, j)],
                outs=[g for g in range(2) if OUT_AT[g] == (u, j) and (n or u)],
                consume=[], consume_out=[], round=[]))
            if last and u == UNITS - 1:
                steps[-1].update(score=None, ready=ready if j == 0 else [])
    for n, s in enumerate(steps):
        for f in s["fills"]:
            steps[n + CONSUME]["consume"].append(f)
            if PROJ_ORDER[f][1] in (1, 3):
                steps[n + ROUND]["round"].append(f)
        for g in s["outs"]:
            steps[n + CONSUME]["consume_out"].append(g)
    return steps


def pair_of(f):
    c, what = PROJ_ORDER[f]
    return 2 * c + what // 2


def macaron(nc, x_in, w_heads, b_heads, wo_t, bv_in, bo_in, rope_in, wr_t, wk_t, wv_t, mu_in, odd_in, out):
    ctx = ExitStack()
    with ctx:
        def sb(name, shape, dt=F32):
            return ctx.enter_context(nc.sbuf_tensor(name, shape, dt))

        def ps(name, shape):
            return ctx.enter_context(nc.psum_tensor(name, shape, F32))

        def sem(name):
            return ctx.enter_context(nc.semaphore(name))

        xn_dram = nc.dram_tensor("xn_scratch", (CHUNKS, P, CHUNK), F32).ap()

        X = sb("X", [P, TILES, E])
        ident = sb("ident", [P, P])
        ident_bf = sb("ident_bf", [P, P], BF16)
        mask_bf = sb("mask_bf", [P, P], BF16)
        ffn_w = sb("ffn_w", [P, 3, P])
        mu = sb("mu", [P, 2])
        odd = sb("odd", [P, CHUNKS])
        bn = sb("bn", [P, TILES, 6])
        mv = sb("mv", [P, TILES, 2])
        var_eps = sb("var_eps", [P, TILES])
        rstd = sb("rstd", [P, TILES])
        neg_half = sb("neg_half", [P, PER_CHUNK])
        eps = sb("eps", [P, PER_CHUNK])
        x_raw = sb("x_raw", [P, CHUNK])
        xs1 = sb("xs1", [P, CHUNK], F32R)
        xs2 = sb("xs2", [P, CHUNK], F32R)
        w_raw = sb("w_raw", [P, W_ALL])
        ws1 = sb("ws1", [P, W_ALL], F32R)
        ws2 = sb("ws2", [P, W_ALL], F32R)
        b_raw = sb("b_raw", [P, 4])
        b_sc = sb("b_sc", [P, 4])
        wo_s = sb("wo_s", [P, QUAD, E])
        rope = sb("rope", [P, 4, S])
        rt = sb("rt", [P, 4, CHUNK])
        parts = sb("parts", [P, 8, S], F32R)
        QS = sb("QS", [P, QUAD, 2, S], F32R)
        KS = sb("KS", [P, QUAD, S], F32R)
        V_next = sb("V_next", [P, QUAD, 8, P], F32R)
        V = sb("V", [P, QUAD, 8, P], F32R)
        probs = sb("probs", [P, P_COLS])
        p1 = sb("p1", [P, 2, CHUNK], F32R)
        p2 = sb("p2", [P, 2, CHUNK], F32R)
        OT = sb("OT", [P, QUAD, S])
        neg_max = sb("neg_max", [P, 8])
        row_sum = sb("row_sum", [P, 8])
        recip = sb("recip", [P, 8])
        XN = rt[:, :, :].rearrange("p a b -> p (a b)").rearrange("p (t e) -> p t e", e=E)
        PAD = CHUNK + 1
        flat_OT = OT[:, :, :].rearrange("p a b -> p (a b)")
        XT = flat_OT[:, 0:1 + CHUNKS * PAD]
        TMP = flat_OT[:, 2560:2560 + CHUNK]
        bias_row = flat_OT[:, 3200:3200 + E]
        wo_all = flat_OT[:, 2560:2560 + 8 * E]
        bv_col = flat_OT[:, 3600:3608]
        bv_wide = flat_OT[:, 3640:3640 + P]
        bo_row = flat_OT[0:1, 3800:3800 + E]
        one_row = flat_OT[0:1, 3930:3930 + P]
        XR = probs[:, 0:CHUNKS * CHUNK]
        XK = probs[:, CHUNKS * CHUNK:2 * CHUNKS * CHUNK]
        flat_rope = rope[:, :, :].rearrange("p a b -> p (a b)")
        KA = flat_rope[:, 0:CHUNKS * CHUNK]
        SG = flat_rope[:, CHUNKS * CHUNK:2 * CHUNKS * CHUNK]
        cbias = sb("cbias", [P, E])

        SC = ps("SC", [P, 2, S])
        TB = ps("TB", [P, 2, CHUNK])
        OM = ps("OM", [P, 2, CHUNK])
        SC4 = SC[:, :, :].rearrange("p a b -> p (a b)")
        OM2 = OM[:, :, :].rearrange("p a b -> p (a b)")
        TB2 = TB[:, :, :].rearrange("p a b -> p (a b)")

        s_x = [sem(f"s_x{c}") for c in range(CHUNKS)]; s_small = sem("s_small"); s_setup = sem("s_setup"); s_ident = sem("s_ident")
        s_bn = sem("s_bn"); s_mv = sem("s_mv"); s_eps = sem("s_eps"); s_rstd = sem("s_rstd")
        s_xn = sem("s_xn"); s_xnt = sem("s_xnt"); s_xt = sem("s_xt"); s_prev = sem("s_prev")
        s_diff = sem("s_diff"); s_mix = sem("s_mix"); s_k = sem("s_k"); s_r = sem("s_r")
        s_relu = sem("s_relu"); s_ka = sem("s_ka"); s_sg = sem("s_sg"); s_v = sem("s_v")
        s_half = sem("s_half"); s_ffn = sem("s_ffn")
        s_bias_in = sem("s_bias_in"); s_bvw = sem("s_bvw"); s_bias_ps = sem("s_bias_ps"); s_bias = sem("s_bias")
        s_biased = sem("s_biased")
        s_scratch = sem("s_scratch"); s_rope_in = sem("s_rope_in"); s_out = sem("s_out")
        s_w_raw = sem("s_w_raw"); s_x_raw = sem("s_x_raw"); s_wo = sem("s_wo")
        s_ws1 = sem("s_ws1"); s_ws2 = sem("s_ws2"); s_xs1 = sem("s_xs1"); s_xs2 = sem("s_xs2")
        s_fill = sem("s_fill"); s_misc = sem("s_misc")
        s_rope = sem("s_rope"); s_radd = sem("s_radd"); s_rnd = sem("s_rnd"); s_sub = sem("s_sub")
        s_v1 = sem("s_v1")
        s_stack = [sem(f"s_stack{h}") for h in range(QUAD)]
        s_vcopy = [sem(f"s_vcopy{h}") for h in range(QUAD)]
        s_scores = sem("s_scores"); s_max = sem("s_max"); s_probs = sem("s_probs")
        s_recip = sem("s_recip"); s_norm = sem("s_norm")
        s_pt = sem("s_pt"); s_p1 = sem("s_p1"); s_p2 = sem("s_p2"); s_av = sem("s_av"); s_ot = sem("s_ot")

        BODY = schedule([1, 2, 3, 4, 5, 6, 7, 0], False)
        HEAD = schedule([0], False)
        TAIL = schedule([1, 2, 3, 4, 5, 6, 7], True)

        def out_no(i, g, last):
            return at(i, 0, FILLS, PROJ + g + (0 if last else PROJ))

        def score_no(i, tile):
            ahead, u, k = tile
            return at(i, ahead, 4 * UNITS, 4 * u + k)

        def block_no(i, ahead, u, j):
            return at(i, ahead, ALL_BLOCKS, BLOCK0[u] + j)

        def probs_of(u, k):
            t = 4 * (u % 2) + k
            return slice(P_OFF[t], P_OFF[t] + TILE_LEN[t]), t

        block = ctx.enter_context(nc.Block())


        @block.sync
        def _(sp):
            x_view = x_in.rearrange("b (t p) e -> p (b t) e", p=P)
            for c in range(CHUNKS):
                sp.dma_start(X[:, 4 * c:4 * c + 4, :], x_view[:, 4 * c:4 * c + 4, :]).then_inc(s_x[c], 16)
            sp.dma_start(ffn_w[:, 0, :], wr_t).then_inc(s_small, 16)
            sp.dma_start(ffn_w[:, 1, :], wk_t).then_inc(s_small, 16)
            sp.dma_start(ffn_w[:, 2, :], wv_t).then_inc(s_small, 16)
            sp.dma_start(mu[:, :], mu_in).then_inc(s_small, 16)
            sp.dma_start(odd[:, :], odd_in).then_inc(s_small, 16)

            sp.dma_start(wo_all.rearrange("p (c e) -> p c e", e=E),
                         wo_t.rearrange("(c p) e -> p c e", p=P)).then_inc(s_bias_in, 16)
            sp.dma_start(bv_col, bv_in).then_inc(s_bias_in, 16)
            sp.dma_start(bo_row, bo_in).then_inc(s_bias_in, 16)

            def load_weights(i):
                sp.dma_start(w_raw[:, :], w_heads[bass.ds(i % QUADS, 1)].rearrange("a p n -> (a p) n")
                             ).then_inc(s_w_raw, 16)
                sp.dma_start(b_raw[:, :], b_heads[bass.ds(i % QUADS, 1)].rearrange("a p n -> (a p) n")
                             ).then_inc(s_w_raw, 16)

            def load_x(i, c):
                sp.dma_start(x_raw[:, :], xn_dram[bass.ds(2 * ((i % ITERS) // QUADS) + c, 1)]
                             .rearrange("a p n -> (a p) n")).then_inc(s_x_raw, 16)

            def load_wo(i):
                for r in range(2):
                    sp.dma_start(wo_s[r * DK:(r + 1) * DK, :, :],
                                 wo_t.rearrange("(q h d) e -> q d h e", q=QUADS, h=QUAD)
                                 [bass.ds(i % QUADS, 1)].rearrange("a d h e -> (a d) h e")).then_inc(s_wo, 16)

            def stack(h):
                rows = slice(HALF * h, HALF * (h + 1))
                for strip, part in enumerate((0, 1, 0, 1)):
                    for half in range(2):
                        sp.dma_start(QS[HALF * strip:HALF * (strip + 1), h, half, :].bitcast(F32),
                                     parts[rows, part + 2 * half, :].bitcast(F32)).then_inc(s_stack[h], 16)
                for strip in range(4):
                    sp.dma_start(KS[HALF * strip:HALF * (strip + 1), h, :].bitcast(F32),
                                 parts[rows, 4 + strip, :].bitcast(F32)).then_inc(s_stack[h], 16)

            load_weights(0)
            for c in range(CHUNKS):
                sp.wait_ge(s_xt, CHUNKS + c + 1)
                sp.dma_start(xn_dram[c], XT[:, 1 + PAD * c + 1:1 + PAD * (c + 1)]).then_inc(s_scratch, 16)
            sp.wait_ge(s_ffn, CHUNKS)
            sp.dma_start(rope[:, :, :], rope_in).then_inc(s_rope_in, 16)
            sp.wait_ge(s_scratch, 16 * CHUNKS)
            load_x(0, 0)
            sp.wait_ge(s_xs2, 1)
            load_x(0, 1)
            sp.wait_ge(s_sub, 8)
            for h in range(QUAD):
                stack(h)
            sp.wait_ge(s_misc, PROJ)
            for h in range(QUAD):
                sp.dma_start(V[:, h, :, :].bitcast(F32), V_next[:, h, :, :].bitcast(F32)).then_inc(s_vcopy[h], 16)
            sp.wait_ge(s_ws2, 4)
            load_weights(1)
            sp.wait_ge(s_xs2, 2)
            load_x(1, 0)

            with sp.Fori(0, ITERS - 1) as i:
                sp.wait_ge(s_fill, i * FILLS + PROJ)
                sp.nop(nofuse=True)
                load_wo(i)
                sp.wait_ge(s_xs2, i * 2 + 3)
                sp.nop(nofuse=True)
                load_x(i + 1, 1)
                for h in range(QUAD):
                    if h == 0:
                        sp.wait_ge(s_sub, i * 8 + 16)
                        sp.nop(nofuse=True)
                        sp.wait_ge(s_misc, i * FILLS + 2 * PROJ)
                        sp.nop(nofuse=True)
                    sp.wait_ge(s_scores, i * 32 + 8 * h + 8)
                    sp.nop(nofuse=True)
                    stack(h)
                    sp.wait_ge(s_av, i * ALL_BLOCKS + BLOCK0[2 * h + 2])
                    sp.nop(nofuse=True)
                    sp.dma_start(V[:, h, :, :].bitcast(F32), V_next[:, h, :, :].bitcast(F32)).then_inc(s_vcopy[h], 16)
                sp.wait_ge(s_ws2, i * 4 + 8)
                sp.nop(nofuse=True)
                load_weights(i + 2)
                sp.wait_ge(s_xs2, i * 2 + 4)
                sp.nop(nofuse=True)
                load_x(i + 2, 0)
            sp.wait_ge(s_fill, (ITERS - 1) * FILLS + PROJ)
            load_wo(ITERS - 1)
            out_view = out.rearrange("b (t p) e -> p (b t) e", p=P)
            for c in range(CHUNKS):
                sp.wait_ge(s_ffn, CHUNKS + c + 1)
                sp.dma_start(out_view[:, 4 * c:4 * c + 4, :], X[:, 4 * c:4 * c + 4, :]).then_inc(s_out, 16)
            sp.wait_ge(s_out, 16 * CHUNKS)

        @block.gpsimd
        def _(pool):
            pool.memset(ident[:, :], 0.0).then_inc(s_setup, 1)
            pool.memset(mask_bf[:, :], 0.0).then_inc(s_setup, 1)
            pool.memset(neg_half[:, :], -0.5).then_inc(s_setup, 1)
            pool.memset(eps[:, :], EPS).then_inc(s_setup, 1)
            pool.memset(XT[:, 0:1], 0.0).then_inc(s_setup, 1)
            pool.memset(one_row, 1.0).then_inc(s_setup, 1)
            pool.wait_ge(s_setup, 6)
            pool.affine_select(out=ident[:, :], in_=ident[:, :], compare_op=ALU.not_equal, fill=1.0, base=0,
                               pattern=[[-1, P]], channel_multiplier=1).then_inc(s_setup, 1)
            pool.affine_select(out=mask_bf[:, :], in_=mask_bf[:, :], compare_op=ALU.is_ge, fill=MASKED, base=0,
                               pattern=[[-1, P]], channel_multiplier=1).then_inc(s_setup, 1)
            pool.wait_ge(s_setup, 8)
            pool.tensor_copy(ident_bf[:, :], ident[:, :]).then_inc(s_ident, 1)

            def norm_scale(n):
                with pool.Fori(0, CHUNKS) as c:
                    pool.wait_ge(s_mv, c * 4 + 16 * n + 4)
                    pool.nop(nofuse=True)
                    pool.tensor_tensor(var_eps[:, bass.ds(c * 4, 4)], mv[:, bass.ds(c * 4, 4), 1], eps[:, :],
                                       ALU.add).then_inc(s_eps, 1)
                    pool.wait_ge(s_eps, c + 4 * n + 1)
                    pool.nop(nofuse=True)
                    pool.tensor_tensor(rstd[:, bass.ds(c * 4, 4)], var_eps[:, bass.ds(c * 4, 4)],
                                       neg_half[:, :], ALU.pow).then_inc(s_rstd, 1)

            def token_shift(n, f):
                pool.wait_ge(s_small, 16 * 5)
                with pool.Fori(0, CHUNKS) as c:
                    pool.wait_ge(s_xt, c + 4 * n + 1)
                    pool.nop(nofuse=True)
                    pool.tensor_tensor(XT[:, bass.ds(c * PAD + 1, 1)], XT[:, bass.ds(c * PAD, 1)],
                                       odd[:, bass.ds(c, 1)], ALU.mult).then_inc(s_prev, 1)
                    pool.wait_ge(s_prev, c + 4 * f + 1)
                    pool.nop(nofuse=True)
                    pool.tensor_tensor(XR[:, bass.ds(c * CHUNK, CHUNK)], XT[:, bass.ds(c * PAD + 2, CHUNK)],
                                       XT[:, bass.ds(c * PAD + 1, CHUNK)], ALU.subtract).then_inc(s_diff, 1)

            norm_scale(0)
            token_shift(0, 0)
            norm_scale(1)
            pool.wait_ge(s_bias, 1)
            with pool.Fori(0, TILES) as t:
                pool.wait_ge(s_xn, t + TILES + 1)
                pool.nop(nofuse=True)
                pool.tensor_tensor(X[:, bass.ds(t, 1), :].rearrange("p a e -> p (a e)"),
                                   X[:, bass.ds(t, 1), :].rearrange("p a e -> p (a e)"),
                                   cbias[:, :], ALU.add).then_inc(s_biased, 1)


            def rotate_add(i, ahead, f, number):
                pool.wait_ge(s_rope, at(i, ahead, 8, 2 * pair_of(f) + 2))
                pool.wait_ge(s_misc, number + 1)
                pool.tensor_tensor(rt[:, 0, :], rt[:, 0, :], rt[:, 3, :], ALU.add).then_inc(s_radd, 1)
                pool.tensor_tensor(rt[:, 2, :], rt[:, 2, :], rt[:, 1, :], ALU.add).then_inc(s_radd, 1)

            def rotate_rest(i, ahead, f):
                c, what = PROJ_ORDER[f]
                base, cols = 4 * (what // 2), slice(c * CHUNK, (c + 1) * CHUNK)
                pool.wait_ge(s_rnd, at(i, ahead, 8, 2 * pair_of(f) + 2))
                for half in range(2):
                    pool.tensor_tensor(parts[:, base + 2 + half, cols], rt[:, 2 * half, :],
                                       parts[:, base + half, cols].bitcast(F32), ALU.subtract).then_inc(s_sub, 1)

            def normalize(i, tile):
                cols, slot = probs_of(*tile[1:])
                pool.wait_ge(s_recip, score_no(i, tile) + 1)
                pool.nop(nofuse=True)
                pool.tensor_scalar(probs[:, cols], probs[:, cols], recip[:, slot:slot + 1], 1.0,
                                   ALU.mult, ALU.mult).then_inc(s_norm, 1)

            def pool_run(i, steps):
                for s in steps:
                    for tile in s["ready"]:
                        normalize(i, tile)
                    for f in s["consume"]:
                        if PROJ_ORDER[f][1] in (1, 3):
                            rotate_add(i, 1, f, at(i, 0, FILLS, PROJ + f))
                    for f in s["round"]:
                        rotate_rest(i, 1, f)

            for f in range(PROJ):
                if PROJ_ORDER[f][1] in (1, 3):
                    rotate_add(0, 0, f, f)
                    rotate_rest(0, 0, f)
            for k in range(4):
                normalize(0, (0, 0, k))
            pool_run(0, HEAD)
            with pool.Fori(0, ITERS - 1) as i:
                pool_run(i, BODY)
            pool_run(ITERS - 1, TAIL)

            norm_scale(2)
            token_shift(2, 1)

        @block.scalar
        def _(act):
            def transposed(n):
                with act.Fori(0, CHUNKS) as c:
                    act.wait_ge(s_xnt, c + 4 * n + 1)
                    act.nop(nofuse=True)
                    act.activation(XT[:, bass.ds(c * PAD + 2, CHUNK)], SC4[:, bass.ds(c * CHUNK, CHUNK)],
                                   ACT.Copy).then_inc(s_xt, 1)

            def gates(f):
                with act.Fori(0, CHUNKS) as c:
                    act.wait_ge(s_k, c + 4 * f + 1)
                    act.nop(nofuse=True)
                    act.activation(KA[:, bass.ds(c * CHUNK, CHUNK)], TB2[:, bass.ds((c % 2) * CHUNK, CHUNK)],
                                   ACT.Relu).then_inc(s_relu, 1)
                    act.wait_ge(s_relu, c + 4 * f + 1)
                    act.nop(nofuse=True)
                    act.activation(KA[:, bass.ds(c * CHUNK, CHUNK)], KA[:, bass.ds(c * CHUNK, CHUNK)],
                                   ACT.Square).then_inc(s_ka, 1)
                    act.wait_ge(s_r, c + 4 * f + 1)
                    act.nop(nofuse=True)
                    act.activation(SG[:, bass.ds(c * CHUNK, CHUNK)], SC4[:, bass.ds(c * CHUNK, CHUNK)],
                                   ACT.Sigmoid).then_inc(s_sg, 1)

            transposed(0)
            gates(0)
            transposed(1)

            def split_weights(i, ahead):
                act.wait_ge(s_w_raw, at(i, ahead, 32, 32))
                act.activation(ws1[:, 0:2 * P], w_raw[:, 0:2 * P], ACT.Copy, scale=SCALE).then_inc(s_ws1, 1)
                act.activation(ws1[:, 2 * P:], w_raw[:, 2 * P:], ACT.Copy).then_inc(s_ws1, 1)

            def split_x(i, ahead, c):
                act.wait_ge(s_x_raw, at(i, ahead, 32, 16 * c + 16))
                act.activation(xs1[:, :], x_raw[:, :], ACT.Copy).then_inc(s_xs1, 1)

            def value_head(i, ahead, f, number):
                c, what = PROJ_ORDER[f]
                act.wait_ge(s_fill, number + 1)
                act.activation(V_next[:, :, 4 * c + what - 4, 0:DK],
                               OM[:, 1, 0:W_V].rearrange("p (h d) -> p h d", h=QUAD), ACT.Copy).then_inc(s_v1, 1)

            def rotate_round(i, ahead, f):
                c, what = PROJ_ORDER[f]
                for half in range(2):
                    act.wait_ge(s_radd, at(i, ahead, 8, 2 * pair_of(f) + half + 1))
                    act.activation(parts[:, 4 * (what // 2) + half, c * CHUNK:(c + 1) * CHUNK], rt[:, 2 * half, :],
                                   ACT.Copy).then_inc(s_rnd, 1)

            def exponentials(i, tile):
                cols, slot = probs_of(*tile[1:])
                n = score_no(i, tile)
                act.wait_ge(s_max, n + 1)
                act.activation(probs[:, cols], SC[:, tile[2] % 2, 0:TILE_LEN[slot]], ACT.Exp,
                               bias=neg_max[:, slot:slot + 1], accum_out=row_sum[:, slot:slot + 1]
                               ).then_inc(s_probs, 1)

            def act_run(i, steps, first=False, last=False):
                for s in steps:
                    ahead, u, j = s["ahead"], s["unit"], s["j"]
                    m = block_no(i, ahead, u, j)
                    slot, cols = (BLOCK0[u] + j) % 2, slice(first_col(u % 2, j), CHUNK)
                    act.wait_ge(s_pt, m + 1)
                    if not first or j >= 2:
                        act.wait_ge(s_av, m - 1)
                    act.activation(p1[:, slot, cols], TB[:, slot, cols], ACT.Copy).then_inc(s_p1, 1)
                    if s["score"]:
                        if s["score"][2] == 0 and not first:
                            act.wait_ge(s_pt, block_no(i, ahead, u, 0))
                        exponentials(i, s["score"])
                    if j == 0 and not first:
                        evacuate(i, ahead, u)
                    for f in s["consume"]:
                        if PROJ_ORDER[f][1] >= 4:
                            value_head(i, 1, f, at(i, 0, FILLS, PROJ + f))
                        if f == 7:
                            act.wait_ge(s_fill, at(i, 0, FILLS, PROJ + 8))
                            split_x(i, 1, 1)
                    for f in s["round"]:
                        if f == 1:
                            for h in range(QUAD):
                                act.wait_ge(s_stack[h], at(i, 0, 192, 192))
                        rotate_round(i, 1, f)
                    if (u, j) == (1, 0) and not last:
                        act.wait_ge(s_fill, at(i, 0, FILLS, PROJ))
                        split_weights(i, 1)
                        split_x(i, 1, 0)
                        for h in range(QUAD):
                            act.wait_ge(s_vcopy[h], at(i, 0, 16, 16))

            def evacuate(i, ahead, u):
                h, g = ((u - 1) % UNITS) // 2, (u - 1) % 2
                act.wait_ge(s_av, block_no(i, ahead, u, 0))
                act.activation(OT[:, h, g * CHUNK:(g + 1) * CHUNK], OM[:, 0, :], ACT.Copy).then_inc(s_ot, 1)

            split_weights(0, 0)
            split_x(0, 0, 0)
            for f in range(PROJ):
                if PROJ_ORDER[f][1] >= 4:
                    value_head(0, 0, f, f)
                if PROJ_ORDER[f][1] in (1, 3):
                    rotate_round(0, 0, f)
                if f == 7:
                    act.wait_ge(s_fill, 8)
                    split_x(0, 0, 1)
            for k in range(4):
                exponentials(0, (0, 0, k))
            act_run(0, HEAD, first=True)
            with act.Fori(0, ITERS - 1) as i:
                act_run(i, BODY)
            act_run(ITERS - 1, TAIL, last=True)
            evacuate(ITERS - 1, 1, 0)

            transposed(2)
            gates(1)

        @block.vector
        def _(dve):
            def norm_input(n, ready):
                for t in range(TILES):
                    if t % PER_CHUNK == 0:
                        ready(t // PER_CHUNK)
                    dve.bn_stats(bn[:, t, :], X[:, t, :]).then_inc(s_bn, 1)
                    if t:
                        dve.wait_ge(s_bn, TILES * n + t)
                        dve.bn_aggr(mv[:, t - 1, :], bn[:, t - 1, :]).then_inc(s_mv, 1)
                dve.wait_ge(s_bn, TILES * n + TILES)
                dve.bn_aggr(mv[:, TILES - 1, :], bn[:, TILES - 1, :]).then_inc(s_mv, 1)
                with dve.Fori(0, CHUNKS) as c:
                    dve.wait_ge(s_rstd, c + 4 * n + 1)
                    for t in range(PER_CHUNK):
                        tile = bass.ds(c * 4 + t, 1)
                        dve.tensor_scalar(XN[:, tile, :].rearrange("p a e -> p (a e)"),
                                          X[:, tile, :].rearrange("p a e -> p (a e)"),
                                          mv[:, tile, 0], rstd[:, tile],
                                          ALU.subtract, ALU.mult).then_inc(s_xn, 1)

            def mix(f):
                with dve.Fori(0, CHUNKS) as c:
                    dve.wait_ge(s_diff, c + 4 * f + 1)
                    here = bass.ds(c * CHUNK, CHUNK)
                    prev = XT[:, bass.ds(c * PAD + 1, CHUNK)]
                    dve.scalar_tensor_tensor(out=XK[:, here], in0=XR[:, here], scalar=mu[:, 1:2], in1=prev,
                                             op0=ALU.mult, op1=ALU.add).then_inc(s_mix, 1)
                    dve.scalar_tensor_tensor(out=XR[:, here], in0=XR[:, here], scalar=mu[:, 0:1], in1=prev,
                                             op0=ALU.mult, op1=ALU.add).then_inc(s_mix, 1)

            def combine(f):
                for c in range(CHUNKS):
                    dve.wait_ge(s_v, 4 * f + c + 1)
                    dve.wait_ge(s_sg, 4 * f + c + 1)
                    if c:
                        dve.wait_ge(s_ffn, 4 * f + c)
                    dve.scalar_tensor_tensor(out=TMP, in0=OM[:, c % 2, :], scalar=0.5,
                                             in1=SG[:, c * CHUNK:(c + 1) * CHUNK], op0=ALU.mult,
                                             op1=ALU.mult).then_inc(s_half, 1)
                    dve.wait_ge(s_half, 4 * f + c + 1)
                    x = X[:, c * 4:c * 4 + 4, :].rearrange("p t e -> p (t e)")
                    dve.tensor_tensor(x, x, TMP, ALU.add).then_inc(s_ffn, 1)

            norm_input(0, lambda c: dve.wait_ge(s_x[c], 16))
            dve.wait_ge(s_bias_ps, 1)
            dve.tensor_copy(cbias[:, :], OM[:, 1, 0:E]).then_inc(s_bias, 1)
            mix(0)
            combine(0)
            norm_input(1, lambda c: dve.wait_ge(s_ffn, c + 1))

            def split_weights(i, ahead):
                dve.wait_ge(s_ws1, at(i, ahead, 2, 2))
                dve.scalar_tensor_tensor(out=ws2[:, 0:2 * P], in0=w_raw[:, 0:2 * P], scalar=SCALE,
                                         in1=ws1[:, 0:2 * P].bitcast(F32), op0=ALU.mult,
                                         op1=ALU.subtract).then_inc(s_ws2, 1)
                dve.tensor_tensor(ws2[:, 2 * P:], w_raw[:, 2 * P:], ws1[:, 2 * P:].bitcast(F32),
                                  ALU.subtract).then_inc(s_ws2, 1)
                dve.tensor_scalar(b_sc[:, 0:2], b_raw[:, 0:2], SCALE, None, ALU.mult).then_inc(s_ws2, 1)
                dve.tensor_copy(b_sc[:, 2:4], b_raw[:, 2:4]).then_inc(s_ws2, 1)
                dve.wait_ge(s_ws2, at(i, ahead, 4, 4))

            def split_x(i, ahead, c):
                dve.wait_ge(s_xs1, at(i, ahead, 2, c + 1))
                dve.tensor_tensor(xs2[:, :], x_raw[:, :], xs1[:, :].bitcast(F32), ALU.subtract).then_inc(s_xs2, 1)

            def rotate(i, ahead, f, number):
                c, what = PROJ_ORDER[f]
                cols = slice(c * CHUNK, (c + 1) * CHUNK)
                dve.wait_ge(s_fill, number + 1)
                if what % 2 == 0 and not (isinstance(i, int) and ahead == 0 and pair_of(f) == 0):
                    dve.wait_ge(s_sub, at(i, ahead, 8, 2 * pair_of(f)))
                for table in (0, 1):
                    product = dve.scalar_tensor_tensor(
                        out=rt[:, 2 * (what % 2) + table, :], in0=OM[:, 1, :], scalar=b_sc[:, what:what + 1],
                        in1=rope[:, [[0, 1], [2, 3]][what % 2][table], cols], op0=ALU.add, op1=ALU.mult)
                    product.then_inc(s_rope if table == 0 else s_misc, 1)

            def value_rest(i, ahead, f, number):
                c, what = PROJ_ORDER[f]
                dve.wait_ge(s_v1, at(i, ahead, 8, 4 * c + what - 4 + 1))
                dve.tensor_tensor(V_next[:, :, 4 * c + what - 4, DK:P],
                                  OM[:, 1, 0:W_V].rearrange("p (h d) -> p h d", h=QUAD),
                                  V_next[:, :, 4 * c + what - 4, 0:DK].bitcast(F32),
                                  ALU.subtract).then_inc(s_misc, 1)

            def maximum(i, tile):
                slot = probs_of(*tile[1:])[1]
                dve.wait_ge(s_scores, score_no(i, tile) + 1)
                dve.tensor_reduce(neg_max[:, slot:slot + 1], SC[:, tile[2] % 2, 0:TILE_LEN[slot]], AX_X, ALU.max,
                                  negate=True).then_inc(s_max, 1)

            def reciprocal(i, tile):
                slot = probs_of(*tile[1:])[1]
                dve.wait_ge(s_probs, score_no(i, tile) + 1)
                dve.reciprocal(recip[:, slot:slot + 1], row_sum[:, slot:slot + 1]).then_inc(s_recip, 1)

            def add_output(i, g, number):
                x = X[:, bass.ds((i // QUADS) * 8 + 4 * g, 4), :].rearrange("p t e -> p (t e)")
                dve.wait_ge(s_fill, number + 1)
                dve.tensor_tensor(x, OM[:, 1, :], x, ALU.add).then_inc(s_misc, 1)

            def dve_run(i, steps, first=False, last=False):
                for s in steps:
                    ahead, u, j = s["ahead"], s["unit"], s["j"]
                    m = block_no(i, ahead, u, j)
                    cols, slot = slice(first_col(u % 2, j), CHUNK), (BLOCK0[u] + j) % 2
                    if j == 0:
                        for tile in s["ready"]:
                            reciprocal(i, tile)
                    dve.wait_ge(s_p1, m + 1)
                    if not first or j >= 2:
                        dve.wait_ge(s_av, m - 1)
                    dve.tensor_tensor(p2[:, slot, cols], TB[:, slot, cols],
                                      p1[:, slot, cols].bitcast(F32),
                                      ALU.subtract).then_inc(s_p2, 1)
                    for tile in s["ready"] if j else []:
                        reciprocal(i, tile)
                    if s["score"]:
                        maximum(i, s["score"])
                    for f in s["consume"]:
                        number = at(i, 0, FILLS, PROJ + f)
                        (rotate if PROJ_ORDER[f][1] < 4 else value_rest)(i, 1, f, number)
                        if f == 7:
                            split_x(i, 1, 1)
                    for g in s["consume_out"]:
                        add_output(i, g, out_no(i, g, last))
                    if (u, j) == (1, 0) and not last:
                        split_weights(i, 1)
                        split_x(i, 1, 0)

            dve.wait_ge(s_rope_in, 16)
            split_weights(0, 0)
            split_x(0, 0, 0)
            for f in range(PROJ):
                (rotate if PROJ_ORDER[f][1] < 4 else value_rest)(0, 0, f, f)
                if f == 7:
                    split_x(0, 0, 1)
            for k in range(4):
                maximum(0, (0, 0, k))
                reciprocal(0, (0, 0, k))
            dve_run(0, HEAD, first=True)
            dve.wait_ge(s_biased, TILES)
            with dve.Fori(0, ITERS - 1) as i:
                dve_run(i, BODY)
            dve_run(ITERS - 1, TAIL, last=True)
            add_output(ITERS - 1, 1, out_no(ITERS - 1, 1, True))

            norm_input(2, lambda c: dve.wait_ge(s_misc, PROJ + FILLS * (ITERS - 1) + 2))
            mix(1)
            combine(1)

        @block.tensor
        def _(pe):
            def transpose_input(n):
                for t in range(TILES):
                    pe.wait_ge(s_xn, TILES * n + t + 1)
                    done = pe.transpose(SC4[:, t * P:(t + 1) * P], XN[:, t, :], ident[:, :])
                    if t % PER_CHUNK == PER_CHUNK - 1:
                        done.then_inc(s_xnt, 1)

            def ffn(f):
                def keys_gates(c):
                    here = slice(c * CHUNK, (c + 1) * CHUNK)
                    pe.wait_ge(s_mix, 8 * f + 2 * c + 2)
                    if c >= 2:
                        pe.wait_ge(s_relu, 4 * f + c - 1)
                    pe.matmul(TB[:, c % 2, :], ffn_w[:, 1, :], XK[:, here], start=True, stop=True).then_inc(s_k, 1)
                    for t in range(PER_CHUNK):
                        tile = slice(c * CHUNK + t * P, c * CHUNK + (t + 1) * P)
                        done = pe.matmul(SC4[:, tile], XR[:, tile], ffn_w[:, 0, :], start=True, stop=True)
                    done.then_inc(s_r, 1)

                def values(c):
                    pe.wait_ge(s_ka, 4 * f + c + 1)
                    if c >= 2:
                        pe.wait_ge(s_half, 4 * f + c - 1)
                    for t in range(PER_CHUNK):
                        done = pe.matmul(OM[:, c % 2, t * P:(t + 1) * P],
                                         KA[:, c * CHUNK + t * P:c * CHUNK + (t + 1) * P], ffn_w[:, 2, :],
                                         start=True, stop=True)
                    done.then_inc(s_v, 1)

                keys_gates(0)
                for c in range(1, CHUNKS):
                    keys_gates(c)
                    values(c - 1)
                values(CHUNKS - 1)

            pe.wait_ge(s_ident, 1)
            pe.wait_ge(s_bias_in, 16 * 3)
            for c in range(8):
                pe.matmul(OM[:, 1, 0:E], bv_col[:, c:c + 1].to_broadcast([P, P]), wo_all[:, c * E:(c + 1) * E],
                          start=(c == 0), stop=False)
            pe.matmul(OM[:, 1, 0:E], one_row, bo_row, start=False, stop=True).then_inc(s_bias_ps, 1)
            transpose_input(0)
            pe.wait_ge(s_small, 16 * 5)
            pe.wait_ge(s_bias, 1)
            ffn(0)
            transpose_input(1)

            def project(i, ahead, f, number):
                c, what = PROJ_ORDER[f]
                if not (isinstance(number, int) and number == 0):
                    pe.wait_ge(s_misc, number)
                pe.wait_ge(s_ws2, at(i, ahead, 4, 4))
                pe.wait_ge(s_xs2, at(i, ahead, 2, c + 1))
                for n, (w, x) in enumerate(((ws1, xs1), (ws1, xs2), (ws2, xs1))):
                    if what < 4:
                        done = pe.matmul(OM[:, 1, :], w[:, what * P:(what + 1) * P], x[:, :],
                                         start=(n == 0), stop=(n == 2))
                    else:
                        done = pe.matmul(OM[:, 1, 0:W_V], x[:, (what - 4) * P:(what - 3) * P], w[:, W_QK:],
                                         start=(n == 0), stop=(n == 2))
                done.then_inc(s_fill, 1)

            def scores(i, tile):
                ahead, u, k = tile
                h, t = u // 2, 4 * (u % 2) + k
                n = score_no(i, tile)
                if k == 0:
                    pe.wait_ge(s_stack[h], at(i, ahead, 192, 192))
                if not (isinstance(n, int) and n < 2):
                    pe.wait_ge(s_probs, n - 1)
                for half in range(2):
                    for c0 in range(0, TILE_LEN[t], CHUNK):
                        c1 = min(c0 + CHUNK, TILE_LEN[t])
                        pe.matmul(SC[:, k % 2, c0:c1], QS[:, h, half, t * P:(t + 1) * P], KS[:, h, c0:c1],
                                  start=(half == 0), stop=(half == 1 and c1 < TILE_LEN[t]))
                pe.matmul(SC[:, k % 2, t * P:(t + 1) * P], ident_bf[:, :], mask_bf[:, :],
                          start=False, stop=True).then_inc(s_scores, 1)

            def transposes(i, ahead, u, j, first):
                m = block_no(i, ahead, u, j)
                if j == 0:
                    pe.wait_ge(s_norm, at(i, ahead, 4 * UNITS, 4 * u + 4))
                if not first or j >= 2:
                    pe.wait_ge(s_p2, m - 1)
                for k in range(first_col(u % 2, j) // P, 4):
                    off = probs_of(u, k)[0].start + j * P
                    done = pe.transpose(TB[:, (BLOCK0[u] + j) % 2, k * P:(k + 1) * P], probs[:, off:off + P],
                                        ident[:, :])
                done.then_inc(s_pt, 1)

            def values(i, ahead, u, j, first=False):
                h, g, m = u // 2, u % 2, block_no(i, ahead, u, j)
                cols = slice(first_col(g, j), CHUNK)
                pe.wait_ge(s_p2, m + 1)
                if j == 0:
                    pe.wait_ge(s_vcopy[h], at(i, ahead, 16, 16))
                    if not first:
                        pe.wait_ge(s_ot, at(i, ahead, UNITS, u))
                pe.matmul(OM[:, 0, cols], V[:, h, j, :], p1[:, (BLOCK0[u] + j) % 2, cols],
                          start=(j == 0), stop=False)
                pe.matmul(OM[:, 0, cols], V[:, h, j, :], p2[:, (BLOCK0[u] + j) % 2, cols],
                          start=False, stop=(j == BLOCKS[g] - 1)).then_inc(s_av, 1)

            def project_out(i, g, number):
                pe.wait_ge(s_misc, number)
                pe.wait_ge(s_wo, at(i, 0, 32, 32))
                pe.wait_ge(s_ot, at(i, 0, UNITS, UNITS - 1 + g))
                for t in range(4):
                    for h in range(QUAD):
                        done = pe.matmul(OM[:, 1, t * P:(t + 1) * P],
                                         OT[:, h, (4 * g + t) * P:(4 * g + t + 1) * P], wo_s[:, h, :],
                                         start=(h == 0), stop=(h == QUAD - 1))
                done.then_inc(s_fill, 1)

            def pe_run(i, steps, first=False, last=False):
                for s in steps:
                    ahead, u, j = s["ahead"], s["unit"], s["j"]
                    transposes(i, ahead, u, j, first)
                    if s["score"]:
                        scores(i, s["score"])
                    if j:
                        values(i, ahead, u, j - 1, first)
                    elif not first:
                        v = (u - 1) % UNITS
                        values(i, ahead - (u == 0), v, BLOCKS[v % 2] - 1)
                    for f in s["fills"]:
                        project(i, 1, f, at(i, 0, FILLS, PROJ + f))
                    for g in s["outs"]:
                        project_out(i, g, out_no(i, g, last))

            for f in range(PROJ):
                project(0, 0, f, f)
            for k in range(4):
                scores(0, (0, 0, k))
            pe_run(0, HEAD, first=True)
            with pe.Fori(0, ITERS - 1) as i:
                pe_run(i, BODY)
            pe_run(ITERS - 1, TAIL, last=True)
            values(ITERS - 1, 0, UNITS - 1, BLOCKS[1] - 1)
            project_out(ITERS - 1, 1, out_no(ITERS - 1, 1, True))

            transpose_input(2)
            ffn(1)


def rotary_tables():
    theta = np.float32(10000.0) ** (np.arange(0, DK, 2, dtype=np.float32) / np.float32(DK))
    freqs = np.arange(S, dtype=np.float32)[:, None] * (np.float32(1.0) / theta)[None, :]
    emb = np.concatenate([freqs, freqs], axis=-1).T
    even, odd = np.tile(emb[0::2], (QUAD, 1)), np.tile(emb[1::2], (QUAD, 1))
    return np.stack([np.cos(even), np.sin(odd), np.cos(odd), -np.sin(even)], axis=1).astype(np.float32)


def kernel(**inputs):
    import concourse.bacc as bacc
    from concourse.bass_utils import run_bass_kernel_spmd

    a = {k: np.asarray(v) for k, v in inputs.items()}

    def halves(w):
        w = w.reshape(QUADS, QUAD, HALF, 2, -1).transpose(0, 3, 1, 2, 4)
        return w.reshape(QUADS, 2, P, -1)

    qk = np.concatenate([halves(a["L0_attn_wq"]), halves(a["L0_attn_wk"])], axis=1)
    qk = qk.transpose(0, 3, 1, 2).reshape(QUADS, E, W_QK)
    wv = a["L0_attn_wv"].reshape(QUADS, W_V, E).transpose(0, 2, 1)
    biases = np.concatenate([halves(a["L0_attn_bq"]), halves(a["L0_attn_bk"])], axis=1)[..., 0]
    odd = np.zeros((P, CHUNKS), np.float32)
    odd[:, 1::2] = 1.0
    arrays = {
        "x": a["L0_attn_x"],
        "w_heads": np.concatenate([qk, wv], axis=2),
        "b_heads": biases.transpose(0, 2, 1),
        "wo_t": a["L0_attn_wo"].T,
        "bv": a["L0_attn_bv"].reshape(8, P).T,
        "bo": a["L0_attn_bo"].reshape(1, E),
        "rope": rotary_tables(),
        "wr_t": a["L0_ffn_W_r"].T,
        "wk_t": a["L0_ffn_W_k"].T,
        "wv_t": a["L0_ffn_W_v"].T,
        "mu": np.stack([a["L0_ffn_mu_r"], a["L0_ffn_mu_k"]], axis=1),
        "odd": odd,
    }
    arrays = {k: np.ascontiguousarray(v) for k, v in arrays.items()}
    nc = bacc.Bacc("TRN2", target_bir_lowering=False, num_devices=1)
    aps = [nc.dram_tensor("in_" + k, v.shape, F32, kind="ExternalInput").ap() for k, v in arrays.items()]
    out = nc.dram_tensor("y", (B, S, E), F32, kind="ExternalOutput").ap()
    macaron(nc, *aps, out)
    result = run_bass_kernel_spmd(nc, [{"in_" + k: v for k, v in arrays.items()}], core_ids=[0])
    return result.results[0]["y"]
```

```python
from contextlib import ExitStack

import numpy as np

import concourse.bass as bass
from concourse import mybir

ALU = mybir.AluOpType
ACT = mybir.ActivationFunctionType
F32 = mybir.dt.float32
F32R = mybir.dt.float32r
BF16 = mybir.dt.bfloat16
AX_X = mybir.AxisListType.X

P = 128
B, S, E = 2, 1024, 128
H, DK = 16, 64
TILES = B * S // P
CHUNK = 512
CHUNKS = B * S // CHUNK
PER_CHUNK = CHUNK // P
QUAD = 4
QUADS = H // QUAD
ITERS = B * QUADS
HALF = DK // 2
EPS = 1e-5
SCALE = 1.0 / 8.0
MASKED = -1e30

W_QK = 4 * P
W_V = QUAD * DK
W_ALL = W_QK + W_V

GROUPS = [(0, 3, 4, 7), (1, 2, 5, 6)]
UNITS = 2 * QUAD
STEPS = [[[(0, 0)], [(1, 1), (5, 3)], [(2, 1), (6, 3)], [(3, 1), (7, 3)], [(4, 2)]],
         [[(0, 0)], [(1, 0)], [(2, 1), (6, 3)], [(3, 2), (4, 2)], [(5, 2)]]]
UNIT_STEPS = len(STEPS[0])
ALL_STEPS = UNITS * UNIT_STEPS
GROUP_BLOCKS = sum(t + 1 for t in GROUPS[0])
P_COLS = 2 * GROUP_BLOCKS * P

PROJ = 16
FILLS = PROJ + 2
PROJ_ORDER = [(0, 0), (0, 1), (0, 4), (0, 2), (0, 3), (0, 5), (0, 6), (0, 7),
              (1, 0), (1, 1), (1, 4), (1, 2), (1, 3), (1, 5), (1, 6), (1, 7)]
FIRST_VALUE = min(f for f, (_, what) in enumerate(PROJ_ORDER) if what >= 4)
CHUNK0_FILLS = sum(c == 0 for c, _ in PROJ_ORDER)
PROJ_AT = [(1, 0), (1, 2), (1, 4), (2, 1), (2, 3), (2, 4), (3, 0), (3, 1),
           (3, 3), (4, 0), (4, 2), (4, 3), (5, 0), (5, 2), (5, 4), (6, 1)]
OUT_AT = [(7, 2), (0, 2)]
SPLIT_AT = (0, 3)
SCORE_TILE = [2, 1, 0]
ROUND = 4


def step_cols(step):
    return sum(4 - k0 for _, k0 in step) * P


def at(i, ahead, per, rest):
    return i * per + (ahead * per + rest)


def schedule(units, last):
    def later(ahead, unit):
        return ahead + unit // UNITS, unit % UNITS

    steps = []
    exp = (1 if units[0] == 0 and len(units) > 1 else 0, units[0] + 1, 3)
    for n, u in enumerate(units):
        ahead = 1 if n and u == 0 else 0
        for j in range(UNIT_STEPS):
            if j < len(SCORE_TILE):
                score = (*later(ahead, u + 1), SCORE_TILE[j])
            else:
                score = (*later(ahead, u + 2), 3) if j == UNIT_STEPS - 1 else None
            if last and score and score[0]:
                score = None
            if last and exp and (exp[1] >= UNITS or exp[0]):
                exp = None
            steps.append(dict(
                ahead=ahead, unit=u, j=j, score=score, exp=exp,
                fills=[] if last else [f for f, place in enumerate(PROJ_AT) if place == (u, j)],
                outs=[g for g in range(2) if OUT_AT[g] == (u, j) and (n or u)],
                round=[]))
            exp = score
    for n, s in enumerate(steps):
        for f in s["fills"]:
            if PROJ_ORDER[f][1] in (1, 3):
                steps[n + ROUND]["round"].append(f)
    return steps


STACK_DMAS = 8


def pair_of(f):
    c, what = PROJ_ORDER[f]
    return 2 * c + what // 2


def macaron(nc, x_in, w_heads, b_heads, wo_t, bv_in, bo_in, rope_in, wr_t, wk_t, wv_t, mu_in, odd_in, out):
    ctx = ExitStack()
    with ctx:
        def sb(name, shape, dt=F32):
            return ctx.enter_context(nc.sbuf_tensor(name, shape, dt))

        def ps(name, shape):
            return ctx.enter_context(nc.psum_tensor(name, shape, F32))

        def sem(name):
            return ctx.enter_context(nc.semaphore(name))

        xn_dram = nc.dram_tensor("xn_scratch", (CHUNKS, P, CHUNK), F32).ap()

        X = sb("X", [P, TILES, E])
        ident = sb("ident", [P, P])
        ident_bf = sb("ident_bf", [P, P], BF16)
        mask_bf = sb("mask_bf", [P, P], BF16)
        ffn_w = sb("ffn_w", [P, 3, P])
        mu = sb("mu", [P, 2])
        odd = sb("odd", [P, CHUNKS])
        bn = sb("bn", [P, TILES, 6])
        mv = sb("mv", [P, TILES, 2])
        var_eps = sb("var_eps", [P, TILES])
        rstd = sb("rstd", [P, TILES])
        neg_half = sb("neg_half", [P, PER_CHUNK])
        eps = sb("eps", [P, PER_CHUNK])
        x_raw = sb("x_raw", [P, CHUNK])
        xs1 = sb("xs1", [P, CHUNK], F32R)
        xs2 = sb("xs2", [P, CHUNK], F32R)
        w_raw = sb("w_raw", [P, W_ALL])
        ws1 = sb("ws1", [P, W_ALL], F32R)
        ws2 = sb("ws2", [P, W_ALL], F32R)
        b_raw = sb("b_raw", [P, 4])
        b_sc = sb("b_sc", [P, 4])
        wo_s = sb("wo_s", [P, QUAD, E])
        rope = sb("rope", [P, 4, S])
        rt = sb("rt", [P, 4, CHUNK])
        parts = sb("parts", [P, 8, S], F32R)
        QS = sb("QS", [P, QUAD, 2, S], F32R)
        KS = sb("KS", [P, QUAD, S], F32R)
        V_next = sb("V_next", [P, QUAD, 8, P], F32R)
        V = sb("V", [P, QUAD, 8, P], F32R)
        probs = sb("probs", [P, P_COLS])
        p1 = sb("p1", [P, 2, CHUNK], F32R)
        p2 = sb("p2", [P, 2, CHUNK], F32R)
        OT = sb("OT", [P, QUAD, S])
        neg_max = sb("neg_max", [P, 8])
        row_sum = sb("row_sum", [P, 8])
        recip = sb("recip", [P, 8])
        XN = rt[:, :, :].rearrange("p a b -> p (a b)").rearrange("p (t e) -> p t e", e=E)
        PAD = CHUNK + 1
        flat_OT = OT[:, :, :].rearrange("p a b -> p (a b)")
        XT = flat_OT[:, 0:1 + CHUNKS * PAD]
        TMP = flat_OT[:, 2560:2560 + CHUNK]
        bias_row = flat_OT[:, 3200:3200 + E]
        wo_all = flat_OT[:, 2560:2560 + 8 * E]
        bv_col = flat_OT[:, 3600:3608]
        bv_wide = flat_OT[:, 3640:3640 + P]
        bo_row = flat_OT[0:1, 3800:3800 + E]
        one_row = flat_OT[0:1, 3930:3930 + P]
        XR = probs[:, 0:CHUNKS * CHUNK]
        XK = probs[:, CHUNKS * CHUNK:2 * CHUNKS * CHUNK]
        flat_rope = rope[:, :, :].rearrange("p a b -> p (a b)")
        KA = flat_rope[:, 0:CHUNKS * CHUNK]
        SG = flat_rope[:, CHUNKS * CHUNK:2 * CHUNKS * CHUNK]
        cbias = sb("cbias", [P, E])

        SC = ps("SC", [P, 2, S])
        TB = ps("TB", [P, 2, CHUNK])
        OM = ps("OM", [P, 2, CHUNK])
        SC4 = SC[:, :, :].rearrange("p a b -> p (a b)")
        OM2 = OM[:, :, :].rearrange("p a b -> p (a b)")
        TB2 = TB[:, :, :].rearrange("p a b -> p (a b)")

        s_x = [sem(f"s_x{c}") for c in range(CHUNKS)]; s_small = sem("s_small"); s_setup = sem("s_setup"); s_ident = sem("s_ident")
        s_bn = sem("s_bn"); s_mv = sem("s_mv"); s_eps = sem("s_eps"); s_rstd = sem("s_rstd")
        s_xn = sem("s_xn"); s_xnt = sem("s_xnt"); s_xt = sem("s_xt"); s_prev = sem("s_prev")
        s_diff = sem("s_diff"); s_mix = sem("s_mix"); s_k = sem("s_k"); s_r = sem("s_r")
        s_relu = sem("s_relu"); s_ka = sem("s_ka"); s_sg = sem("s_sg"); s_v = sem("s_v")
        s_half = sem("s_half"); s_ffn = sem("s_ffn")
        s_bias_in = sem("s_bias_in"); s_bvw = sem("s_bvw"); s_bias_ps = sem("s_bias_ps"); s_bias = sem("s_bias")
        s_biased = sem("s_biased")
        s_scratch = sem("s_scratch"); s_rope_in = sem("s_rope_in"); s_out = sem("s_out")
        s_w_raw = sem("s_w_raw"); s_x_raw = sem("s_x_raw"); s_wo = sem("s_wo")
        s_ws1 = sem("s_ws1"); s_ws2 = sem("s_ws2"); s_xs1 = sem("s_xs1"); s_xs2 = sem("s_xs2")
        s_fill = sem("s_fill"); s_misc = sem("s_misc")
        s_rope = sem("s_rope"); s_radd = sem("s_radd"); s_rnd = sem("s_rnd"); s_sub = sem("s_sub")
        s_v1 = sem("s_v1")
        s_stack = [sem(f"s_stack{h}") for h in range(QUAD)]
        s_vcopy = [sem(f"s_vcopy{h}") for h in range(QUAD)]
        s_scores = sem("s_scores"); s_max = sem("s_max"); s_probs = sem("s_probs")
        s_recip = sem("s_recip"); s_norm = sem("s_norm")
        s_pt = sem("s_pt"); s_p1 = sem("s_p1"); s_p2 = sem("s_p2"); s_av = sem("s_av"); s_ot = sem("s_ot")

        BODY = schedule([1, 2, 3, 4, 5, 6, 7, 0], False)
        HEAD = schedule([0], False)
        TAIL = schedule([1, 2, 3, 4, 5, 6, 7], True)

        def out_no(i, g, last):
            return at(i, 0, FILLS, PROJ + g + (0 if last else PROJ))

        def score_no(i, tile):
            ahead, u, k = tile
            return at(i, ahead, 4 * UNITS, 4 * u + 3 - k)

        def step_no(i, ahead, u, j):
            return at(i, ahead, ALL_STEPS, UNIT_STEPS * u + j)

        def probs_of(u, k):
            group = GROUPS[u % 2]
            start = ((u % 2) * GROUP_BLOCKS + sum(t + 1 for t in group[:k])) * P
            return slice(start, start + (group[k] + 1) * P), group[k]

        block = ctx.enter_context(nc.Block())


        @block.sync
        def _(sp):
            x_view = x_in.rearrange("b (t p) e -> p (b t) e", p=P)
            for c in range(CHUNKS):
                sp.dma_start(X[:, 4 * c:4 * c + 4, :], x_view[:, 4 * c:4 * c + 4, :]).then_inc(s_x[c], 16)
            sp.dma_start(ffn_w[:, 0, :], wr_t).then_inc(s_small, 16)
            sp.dma_start(ffn_w[:, 1, :], wk_t).then_inc(s_small, 16)
            sp.dma_start(ffn_w[:, 2, :], wv_t).then_inc(s_small, 16)
            sp.dma_start(mu[:, :], mu_in).then_inc(s_small, 16)
            sp.dma_start(odd[:, :], odd_in).then_inc(s_small, 16)

            sp.dma_start(wo_all.rearrange("p (c e) -> p c e", e=E),
                         wo_t.rearrange("(c p) e -> p c e", p=P)).then_inc(s_bias_in, 16)
            sp.dma_start(bv_col, bv_in).then_inc(s_bias_in, 16)
            sp.dma_start(bo_row, bo_in).then_inc(s_bias_in, 16)

            def load_weights(i):
                sp.dma_start(w_raw[:, :], w_heads[bass.ds(i % QUADS, 1)].rearrange("a p n -> (a p) n")
                             ).then_inc(s_w_raw, 16)
                sp.dma_start(b_raw[:, :], b_heads[bass.ds(i % QUADS, 1)].rearrange("a p n -> (a p) n")
                             ).then_inc(s_w_raw, 16)

            def load_x(i, c):
                sp.dma_start(x_raw[:, :], xn_dram[bass.ds(2 * ((i % ITERS) // QUADS) + c, 1)]
                             .rearrange("a p n -> (a p) n")).then_inc(s_x_raw, 16)

            def load_wo(i):
                for r in range(2):
                    sp.dma_start(wo_s[r * DK:(r + 1) * DK, :, :],
                                 wo_t.rearrange("(q h d) e -> q d h e", q=QUADS, h=QUAD)
                                 [bass.ds(i % QUADS, 1)].rearrange("a d h e -> (a d) h e")).then_inc(s_wo, 16)

            def stack_queries(h):
                rows = slice(HALF * h, HALF * (h + 1))
                for strip, part in enumerate((0, 1, 0, 1)):
                    sp.dma_start(QS[HALF * strip:HALF * (strip + 1), h, :, :].bitcast(F32),
                                 parts[rows, part:part + 3:2, :].bitcast(F32)).then_inc(s_stack[h], 16)

            def stack_keys(h):
                rows = slice(HALF * h, HALF * (h + 1))
                for strip in range(4):
                    sp.dma_start(KS[HALF * strip:HALF * (strip + 1), h, :].bitcast(F32),
                                 parts[rows, 4 + strip, :].bitcast(F32)).then_inc(s_stack[h], 16)

            load_weights(0)
            for c in range(CHUNKS):
                sp.wait_ge(s_xt, CHUNKS + c + 1)
                sp.dma_start(xn_dram[c], XT[:, 1 + PAD * c + 1:1 + PAD * (c + 1)]).then_inc(s_scratch, 16)
            sp.wait_ge(s_ffn, CHUNKS)
            sp.dma_start(rope[:, :, :], rope_in).then_inc(s_rope_in, 16)
            sp.wait_ge(s_scratch, 16 * CHUNKS)
            load_x(0, 0)
            sp.wait_ge(s_xs2, 1)
            load_x(0, 1)
            sp.wait_ge(s_sub, 8)
            for h in range(QUAD):
                stack_queries(h)
                stack_keys(h)
            sp.wait_ge(s_misc, PROJ)
            for h in range(QUAD):
                sp.dma_start(V[:, h, :, :].bitcast(F32), V_next[:, h, :, :].bitcast(F32)).then_inc(s_vcopy[h], 16)
            sp.wait_ge(s_ws2, 4)
            load_weights(1)
            sp.wait_ge(s_xs2, 2)
            load_x(1, 0)

            with sp.Fori(0, ITERS - 1) as i:
                sp.wait_ge(s_fill, i * FILLS + PROJ)
                sp.nop(nofuse=True)
                load_wo(i)
                sp.wait_ge(s_xs2, i * 2 + 3)
                sp.nop(nofuse=True)
                load_x(i + 1, 1)
                for h in range(QUAD):
                    if h == 0:
                        sp.wait_ge(s_sub, i * 8 + 14)
                        sp.nop(nofuse=True)
                    if h == QUAD - 1:
                        sp.wait_ge(s_ws2, i * 4 + 8)
                        sp.nop(nofuse=True)
                        load_weights(i + 2)
                        sp.wait_ge(s_xs2, i * 2 + 4)
                        sp.nop(nofuse=True)
                        load_x(i + 2, 0)
                    sp.wait_ge(s_scores, i * 32 + 8 * h + 8)
                    sp.nop(nofuse=True)
                    stack_queries(h)
                    if h == 0:
                        sp.wait_ge(s_sub, i * 8 + 16)
                        sp.nop(nofuse=True)
                    stack_keys(h)
                sp.wait_ge(s_misc, i * FILLS + 2 * PROJ)
                sp.nop(nofuse=True)
                for h in range(QUAD):
                    sp.wait_ge(s_av, i * ALL_STEPS + 2 * UNIT_STEPS * (h + 1))
                    sp.nop(nofuse=True)
                    sp.dma_start(V[:, h, :, :].bitcast(F32), V_next[:, h, :, :].bitcast(F32)).then_inc(s_vcopy[h], 16)
            sp.wait_ge(s_fill, (ITERS - 1) * FILLS + PROJ)
            load_wo(ITERS - 1)
            out_view = out.rearrange("b (t p) e -> p (b t) e", p=P)
            for c in range(CHUNKS):
                sp.wait_ge(s_ffn, CHUNKS + c + 1)
                sp.dma_start(out_view[:, 4 * c:4 * c + 4, :], X[:, 4 * c:4 * c + 4, :]).then_inc(s_out, 16)
            sp.wait_ge(s_out, 16 * CHUNKS)

        @block.gpsimd
        def _(pool):
            pool.memset(ident[:, :], 0.0).then_inc(s_setup, 1)
            pool.memset(mask_bf[:, :], 0.0).then_inc(s_setup, 1)
            pool.memset(neg_half[:, :], -0.5).then_inc(s_setup, 1)
            pool.memset(eps[:, :], EPS).then_inc(s_setup, 1)
            pool.memset(XT[:, 0:1], 0.0).then_inc(s_setup, 1)
            pool.memset(one_row, 1.0).then_inc(s_setup, 1)
            pool.wait_ge(s_setup, 6)
            pool.affine_select(out=ident[:, :], in_=ident[:, :], compare_op=ALU.not_equal, fill=1.0, base=0,
                               pattern=[[-1, P]], channel_multiplier=1).then_inc(s_setup, 1)
            pool.affine_select(out=mask_bf[:, :], in_=mask_bf[:, :], compare_op=ALU.is_ge, fill=MASKED, base=0,
                               pattern=[[-1, P]], channel_multiplier=1).then_inc(s_setup, 1)
            pool.wait_ge(s_setup, 8)
            pool.tensor_copy(ident_bf[:, :], ident[:, :]).then_inc(s_ident, 1)

            def norm_scale(n):
                with pool.Fori(0, CHUNKS) as c:
                    pool.wait_ge(s_mv, c * 4 + 16 * n + 4)
                    pool.nop(nofuse=True)
                    pool.tensor_tensor(var_eps[:, bass.ds(c * 4, 4)], mv[:, bass.ds(c * 4, 4), 1], eps[:, :],
                                       ALU.add).then_inc(s_eps, 1)
                    pool.wait_ge(s_eps, c + 4 * n + 1)
                    pool.nop(nofuse=True)
                    pool.tensor_tensor(rstd[:, bass.ds(c * 4, 4)], var_eps[:, bass.ds(c * 4, 4)],
                                       neg_half[:, :], ALU.pow).then_inc(s_rstd, 1)

            def token_shift(n, f):
                pool.wait_ge(s_small, 16 * 5)
                with pool.Fori(0, CHUNKS) as c:
                    pool.wait_ge(s_xt, c + 4 * n + 1)
                    pool.nop(nofuse=True)
                    pool.tensor_tensor(XT[:, bass.ds(c * PAD + 1, 1)], XT[:, bass.ds(c * PAD, 1)],
                                       odd[:, bass.ds(c, 1)], ALU.mult).then_inc(s_prev, 1)
                    pool.wait_ge(s_prev, c + 4 * f + 1)
                    pool.nop(nofuse=True)
                    pool.tensor_tensor(XR[:, bass.ds(c * CHUNK, CHUNK)], XT[:, bass.ds(c * PAD + 2, CHUNK)],
                                       XT[:, bass.ds(c * PAD + 1, CHUNK)], ALU.subtract).then_inc(s_diff, 1)

            norm_scale(0)
            token_shift(0, 0)
            norm_scale(1)
            pool.wait_ge(s_bias, 1)
            with pool.Fori(0, TILES) as t:
                pool.wait_ge(s_xn, t + TILES + 1)
                pool.nop(nofuse=True)
                pool.tensor_tensor(X[:, bass.ds(t, 1), :].rearrange("p a e -> p (a e)"),
                                   X[:, bass.ds(t, 1), :].rearrange("p a e -> p (a e)"),
                                   cbias[:, :], ALU.add).then_inc(s_biased, 1)


            def rotate_add(i, ahead, f, number):
                a = pair_of(f) % 2
                pool.wait_ge(s_rope, at(i, ahead, 8, 2 * pair_of(f) + 2))
                pool.wait_ge(s_misc, number + 1)
                pool.tensor_tensor(rt[:, a, :], rt[:, a, :], rt[:, 1 - a, :], ALU.add).then_inc(s_radd, 1)
                pool.tensor_tensor(rt[:, 2 + a, :], rt[:, 2 + a, :], rt[:, 3 - a, :], ALU.add).then_inc(s_radd, 1)

            def rotate_rest(i, ahead, f):
                c, what = PROJ_ORDER[f]
                base, cols = 4 * (what // 2), slice(c * CHUNK, (c + 1) * CHUNK)
                pool.wait_ge(s_rnd, at(i, ahead, 8, 2 * pair_of(f) + 2))
                for half in range(2):
                    pool.tensor_tensor(parts[:, base + 2 + half, cols], rt[:, 2 * half + pair_of(f) % 2, :],
                                       parts[:, base + half, cols].bitcast(F32), ALU.subtract).then_inc(s_sub, 1)

            def normalize(i, tile):
                cols, slot = probs_of(*tile[1:])
                pool.wait_ge(s_recip, score_no(i, tile) + 1)
                pool.nop(nofuse=True)
                pool.tensor_scalar(probs[:, cols], probs[:, cols], recip[:, slot:slot + 1], 1.0,
                                   ALU.mult, ALU.mult).then_inc(s_norm, 1)

            def pool_run(i, steps):
                for s in steps:
                    if s["exp"]:
                        normalize(i, s["exp"])
                    for f in s["fills"]:
                        if PROJ_ORDER[f][1] in (1, 3):
                            rotate_add(i, 1, f, at(i, 0, FILLS, PROJ + f))
                    for f in s["round"]:
                        rotate_rest(i, 1, f)

            for f in range(PROJ):
                if PROJ_ORDER[f][1] in (1, 3):
                    rotate_add(0, 0, f, f)
                    rotate_rest(0, 0, f)
            for k in (3, 2, 1, 0):
                normalize(0, (0, 0, k))
            pool_run(0, HEAD)
            with pool.Fori(0, ITERS - 1) as i:
                pool_run(i, BODY)
            pool_run(ITERS - 1, TAIL)

            norm_scale(2)
            token_shift(2, 1)

        @block.scalar
        def _(act):
            def transposed(n):
                with act.Fori(0, CHUNKS) as c:
                    act.wait_ge(s_xnt, c + 4 * n + 1)
                    act.nop(nofuse=True)
                    act.activation(XT[:, bass.ds(c * PAD + 2, CHUNK)], SC4[:, bass.ds(c * CHUNK, CHUNK)],
                                   ACT.Copy).then_inc(s_xt, 1)

            def gates(f):
                with act.Fori(0, CHUNKS) as c:
                    act.wait_ge(s_k, c + 4 * f + 1)
                    act.nop(nofuse=True)
                    act.activation(KA[:, bass.ds(c * CHUNK, CHUNK)], TB2[:, bass.ds((c % 2) * CHUNK, CHUNK)],
                                   ACT.Relu).then_inc(s_relu, 1)
                    act.wait_ge(s_relu, c + 4 * f + 1)
                    act.nop(nofuse=True)
                    act.activation(KA[:, bass.ds(c * CHUNK, CHUNK)], KA[:, bass.ds(c * CHUNK, CHUNK)],
                                   ACT.Square).then_inc(s_ka, 1)
                    act.wait_ge(s_r, c + 4 * f + 1)
                    act.nop(nofuse=True)
                    act.activation(SG[:, bass.ds(c * CHUNK, CHUNK)], SC4[:, bass.ds(c * CHUNK, CHUNK)],
                                   ACT.Sigmoid).then_inc(s_sg, 1)

            transposed(0)
            gates(0)
            transposed(1)

            def split_weights(i, ahead):
                act.wait_ge(s_w_raw, at(i, ahead, 32, 32))
                act.activation(ws1[:, 0:2 * P], w_raw[:, 0:2 * P], ACT.Copy, scale=SCALE).then_inc(s_ws1, 1)
                act.activation(ws1[:, 2 * P:], w_raw[:, 2 * P:], ACT.Copy).then_inc(s_ws1, 1)

            def split_x(i, ahead, c):
                act.wait_ge(s_x_raw, at(i, ahead, 32, 16 * c + 16))
                act.activation(xs1[:, :], x_raw[:, :], ACT.Copy).then_inc(s_xs1, 1)

            def value_head(i, ahead, f, number):
                c, what = PROJ_ORDER[f]
                act.wait_ge(s_fill, number + 1)
                act.activation(V_next[:, :, 4 * c + what - 4, 0:DK],
                               OM[:, 1, 0:W_V].rearrange("p (h d) -> p h d", h=QUAD), ACT.Copy).then_inc(s_v1, 1)

            def rotate_round(i, ahead, f):
                c, what = PROJ_ORDER[f]
                for half in range(2):
                    act.wait_ge(s_radd, at(i, ahead, 8, 2 * pair_of(f) + half + 1))
                    act.activation(parts[:, 4 * (what // 2) + half, c * CHUNK:(c + 1) * CHUNK],
                                   rt[:, 2 * half + pair_of(f) % 2, :], ACT.Copy).then_inc(s_rnd, 1)

            def exponentials(i, tile):
                cols, slot = probs_of(*tile[1:])
                n = score_no(i, tile)
                act.wait_ge(s_max, n + 1)
                act.activation(probs[:, cols], SC[:, (3 - tile[2]) % 2, 0:(slot + 1) * P], ACT.Exp,
                               bias=neg_max[:, slot:slot + 1], accum_out=row_sum[:, slot:slot + 1]
                               ).then_inc(s_probs, 1)

            def act_run(i, steps, first=False, last=False):
                for s in steps:
                    ahead, u, j = s["ahead"], s["unit"], s["j"]
                    m = step_no(i, ahead, u, j)
                    slot, cols = (UNIT_STEPS * u + j) % 2, slice(0, step_cols(STEPS[u % 2][j]))
                    act.wait_ge(s_pt, m + 1)
                    if not first or j >= 2:
                        act.wait_ge(s_av, m - 1)
                    act.activation(p1[:, slot, cols], TB[:, slot, cols], ACT.Copy).then_inc(s_p1, 1)
                    if s["exp"]:
                        exponentials(i, s["exp"])
                    for f in s["fills"]:
                        if f == FIRST_VALUE:
                            for h in range(QUAD):
                                act.wait_ge(s_vcopy[h], at(i, 0, 16, 16))
                        if PROJ_ORDER[f][1] >= 4:
                            value_head(i, 1, f, at(i, 0, FILLS, PROJ + f))
                        if f == CHUNK0_FILLS - 1:
                            act.wait_ge(s_fill, at(i, 0, FILLS, PROJ + CHUNK0_FILLS))
                            split_x(i, 1, 1)
                    for f in s["round"]:
                        if f == 1:
                            for h in range(QUAD):
                                act.wait_ge(s_stack[h], at(i, 0, STACK_DMAS * 16, STACK_DMAS * 16))
                        rotate_round(i, 1, f)
                    if (u, j) == SPLIT_AT:
                        act.wait_ge(s_fill, PROJ if first else at(i, 0, FILLS, 2 * PROJ))
                        split_weights(i, ahead + 1)
                        split_x(i, ahead + 1, 0)
                    if j == 0 and not first:
                        evacuate(i, ahead, u)

            def evacuate(i, ahead, u):
                h, g = ((u - 1) % UNITS) // 2, (u - 1) % 2
                act.wait_ge(s_av, step_no(i, ahead, u, 0))
                act.activation(OT[:, h, g * CHUNK:(g + 1) * CHUNK], OM[:, 0, :], ACT.Copy).then_inc(s_ot, 1)

            split_weights(0, 0)
            split_x(0, 0, 0)
            for f in range(PROJ):
                if PROJ_ORDER[f][1] >= 4:
                    value_head(0, 0, f, f)
                if PROJ_ORDER[f][1] in (1, 3):
                    rotate_round(0, 0, f)
                if f == CHUNK0_FILLS - 1:
                    act.wait_ge(s_fill, CHUNK0_FILLS)
                    split_x(0, 0, 1)
            for k in (3, 2, 1, 0):
                exponentials(0, (0, 0, k))
            act_run(0, HEAD, first=True)
            with act.Fori(0, ITERS - 1) as i:
                act_run(i, BODY)
            act_run(ITERS - 1, TAIL, last=True)
            evacuate(ITERS - 1, 1, 0)

            transposed(2)
            gates(1)

        @block.vector
        def _(dve):
            def norm_input(n, ready):
                for t in range(TILES):
                    if t % PER_CHUNK == 0:
                        ready(t // PER_CHUNK)
                    dve.bn_stats(bn[:, t, :], X[:, t, :]).then_inc(s_bn, 1)
                    if t:
                        dve.wait_ge(s_bn, TILES * n + t)
                        dve.bn_aggr(mv[:, t - 1, :], bn[:, t - 1, :]).then_inc(s_mv, 1)
                dve.wait_ge(s_bn, TILES * n + TILES)
                dve.bn_aggr(mv[:, TILES - 1, :], bn[:, TILES - 1, :]).then_inc(s_mv, 1)
                with dve.Fori(0, CHUNKS) as c:
                    dve.wait_ge(s_rstd, c + 4 * n + 1)
                    for t in range(PER_CHUNK):
                        tile = bass.ds(c * 4 + t, 1)
                        dve.tensor_scalar(XN[:, tile, :].rearrange("p a e -> p (a e)"),
                                          X[:, tile, :].rearrange("p a e -> p (a e)"),
                                          mv[:, tile, 0], rstd[:, tile],
                                          ALU.subtract, ALU.mult).then_inc(s_xn, 1)

            def mix(f):
                with dve.Fori(0, CHUNKS) as c:
                    dve.wait_ge(s_diff, c + 4 * f + 1)
                    here = bass.ds(c * CHUNK, CHUNK)
                    prev = XT[:, bass.ds(c * PAD + 1, CHUNK)]
                    dve.scalar_tensor_tensor(out=XK[:, here], in0=XR[:, here], scalar=mu[:, 1:2], in1=prev,
                                             op0=ALU.mult, op1=ALU.add).then_inc(s_mix, 1)
                    dve.scalar_tensor_tensor(out=XR[:, here], in0=XR[:, here], scalar=mu[:, 0:1], in1=prev,
                                             op0=ALU.mult, op1=ALU.add).then_inc(s_mix, 1)

            def combine(f):
                for c in range(CHUNKS):
                    dve.wait_ge(s_v, 4 * f + c + 1)
                    dve.wait_ge(s_sg, 4 * f + c + 1)
                    if c:
                        dve.wait_ge(s_ffn, 4 * f + c)
                    dve.scalar_tensor_tensor(out=TMP, in0=OM[:, c % 2, :], scalar=0.5,
                                             in1=SG[:, c * CHUNK:(c + 1) * CHUNK], op0=ALU.mult,
                                             op1=ALU.mult).then_inc(s_half, 1)
                    dve.wait_ge(s_half, 4 * f + c + 1)
                    x = X[:, c * 4:c * 4 + 4, :].rearrange("p t e -> p (t e)")
                    dve.tensor_tensor(x, x, TMP, ALU.add).then_inc(s_ffn, 1)

            norm_input(0, lambda c: dve.wait_ge(s_x[c], 16))
            dve.wait_ge(s_bias_ps, 1)
            dve.tensor_copy(cbias[:, :], OM[:, 1, 0:E]).then_inc(s_bias, 1)
            mix(0)
            combine(0)
            norm_input(1, lambda c: dve.wait_ge(s_ffn, c + 1))

            def split_weights(i, ahead):
                dve.wait_ge(s_ws1, at(i, ahead, 2, 2))
                dve.scalar_tensor_tensor(out=ws2[:, 0:2 * P], in0=w_raw[:, 0:2 * P], scalar=SCALE,
                                         in1=ws1[:, 0:2 * P].bitcast(F32), op0=ALU.mult,
                                         op1=ALU.subtract).then_inc(s_ws2, 1)
                dve.tensor_tensor(ws2[:, 2 * P:], w_raw[:, 2 * P:], ws1[:, 2 * P:].bitcast(F32),
                                  ALU.subtract).then_inc(s_ws2, 1)
                dve.tensor_scalar(b_sc[:, 0:2], b_raw[:, 0:2], SCALE, None, ALU.mult).then_inc(s_ws2, 1)
                dve.tensor_copy(b_sc[:, 2:4], b_raw[:, 2:4]).then_inc(s_ws2, 1)
                dve.wait_ge(s_ws2, at(i, ahead, 4, 4))

            def split_x(i, ahead, c):
                dve.wait_ge(s_xs1, at(i, ahead, 2, c + 1))
                dve.tensor_tensor(xs2[:, :], x_raw[:, :], xs1[:, :].bitcast(F32), ALU.subtract).then_inc(s_xs2, 1)

            def rotate(i, ahead, f, number):
                c, what = PROJ_ORDER[f]
                cols = slice(c * CHUNK, (c + 1) * CHUNK)
                dve.wait_ge(s_fill, number + 1)
                a, odd_half = pair_of(f) % 2, what % 2
                if not (isinstance(i, int) and ahead == 0 and pair_of(f) == 0):
                    dve.wait_ge(s_sub if odd_half else s_radd, at(i, ahead, 8, 2 * pair_of(f)))
                places = (3 - a, 1 - a) if odd_half else (a, 2 + a)
                for table in (0, 1):
                    product = dve.scalar_tensor_tensor(
                        out=rt[:, places[table], :], in0=OM[:, 1, :], scalar=b_sc[:, what:what + 1],
                        in1=rope[:, [[0, 1], [2, 3]][what % 2][table], cols], op0=ALU.add, op1=ALU.mult)
                    product.then_inc(s_rope if table == 0 else s_misc, 1)

            def value_rest(i, ahead, f, number):
                c, what = PROJ_ORDER[f]
                dve.wait_ge(s_v1, at(i, ahead, 8, 4 * c + what - 4 + 1))
                dve.tensor_tensor(V_next[:, :, 4 * c + what - 4, DK:P],
                                  OM[:, 1, 0:W_V].rearrange("p (h d) -> p h d", h=QUAD),
                                  V_next[:, :, 4 * c + what - 4, 0:DK].bitcast(F32),
                                  ALU.subtract).then_inc(s_misc, 1)

            def maximum(i, tile):
                slot = probs_of(*tile[1:])[1]
                dve.wait_ge(s_scores, score_no(i, tile) + 1)
                dve.tensor_reduce(neg_max[:, slot:slot + 1], SC[:, (3 - tile[2]) % 2, 0:(slot + 1) * P], AX_X, ALU.max,
                                  negate=True).then_inc(s_max, 1)

            def reciprocal(i, tile):
                slot = probs_of(*tile[1:])[1]
                dve.wait_ge(s_probs, score_no(i, tile) + 1)
                dve.reciprocal(recip[:, slot:slot + 1], row_sum[:, slot:slot + 1]).then_inc(s_recip, 1)

            def add_output(i, g, number):
                tiles = X[:, :, :].rearrange("p (b a t) e -> p b a t e", b=B, t=4)[:, bass.ds(i // QUADS, 1)]
                x = tiles.rearrange("p b a t e -> p (b a) t e")[:, :, slice(0, 4, 3) if g == 0 else slice(1, 3), :]
                dve.wait_ge(s_fill, number + 1)
                dve.tensor_tensor(x, OM[:, 1, :].rearrange("p (a t e) -> p a t e", a=2, t=2), x,
                                  ALU.add).then_inc(s_misc, 1)

            def dve_run(i, steps, first=False, last=False):
                for s in steps:
                    ahead, u, j = s["ahead"], s["unit"], s["j"]
                    m = step_no(i, ahead, u, j)
                    slot, cols = (UNIT_STEPS * u + j) % 2, slice(0, step_cols(STEPS[u % 2][j]))
                    dve.wait_ge(s_p1, m + 1)
                    if not first or j >= 2:
                        dve.wait_ge(s_av, m - 1)
                    dve.tensor_tensor(p2[:, slot, cols], TB[:, slot, cols], p1[:, slot, cols].bitcast(F32),
                                      ALU.subtract).then_inc(s_p2, 1)
                    if s["score"]:
                        maximum(i, s["score"])
                    if s["exp"]:
                        reciprocal(i, s["exp"])
                    for f in s["fills"]:
                        number = at(i, 0, FILLS, PROJ + f)
                        (rotate if PROJ_ORDER[f][1] < 4 else value_rest)(i, 1, f, number)
                        if f == CHUNK0_FILLS - 1:
                            split_x(i, 1, 1)
                    for g in s["outs"]:
                        add_output(i, g, out_no(i, g, last))
                    if (u, j) == SPLIT_AT:
                        split_weights(i, ahead + 1)
                        split_x(i, ahead + 1, 0)

            dve.wait_ge(s_rope_in, 16)
            split_weights(0, 0)
            split_x(0, 0, 0)
            for f in range(PROJ):
                (rotate if PROJ_ORDER[f][1] < 4 else value_rest)(0, 0, f, f)
                if f == CHUNK0_FILLS - 1:
                    split_x(0, 0, 1)
            for k in (3, 2, 1, 0):
                maximum(0, (0, 0, k))
                reciprocal(0, (0, 0, k))
            maximum(0, (0, 1, 3))
            dve_run(0, HEAD, first=True)
            dve.wait_ge(s_biased, TILES)
            with dve.Fori(0, ITERS - 1) as i:
                dve_run(i, BODY)
            dve_run(ITERS - 1, TAIL, last=True)
            add_output(ITERS - 1, 1, out_no(ITERS - 1, 1, True))

            norm_input(2, lambda c: dve.wait_ge(s_misc, PROJ + FILLS * (ITERS - 1) + 2))
            mix(1)
            combine(1)

        @block.tensor
        def _(pe):
            def transpose_input(n):
                for t in range(TILES):
                    pe.wait_ge(s_xn, TILES * n + t + 1)
                    done = pe.transpose(SC4[:, t * P:(t + 1) * P], XN[:, t, :], ident[:, :])
                    if t % PER_CHUNK == PER_CHUNK - 1:
                        done.then_inc(s_xnt, 1)

            def ffn(f):
                def keys_gates(c):
                    here = slice(c * CHUNK, (c + 1) * CHUNK)
                    pe.wait_ge(s_mix, 8 * f + 2 * c + 2)
                    if c >= 2:
                        pe.wait_ge(s_relu, 4 * f + c - 1)
                    pe.matmul(TB[:, c % 2, :], ffn_w[:, 1, :], XK[:, here], start=True, stop=True).then_inc(s_k, 1)
                    for t in range(PER_CHUNK):
                        tile = slice(c * CHUNK + t * P, c * CHUNK + (t + 1) * P)
                        done = pe.matmul(SC4[:, tile], XR[:, tile], ffn_w[:, 0, :], start=True, stop=True)
                    done.then_inc(s_r, 1)

                def values(c):
                    pe.wait_ge(s_ka, 4 * f + c + 1)
                    if c >= 2:
                        pe.wait_ge(s_half, 4 * f + c - 1)
                    for t in range(PER_CHUNK):
                        done = pe.matmul(OM[:, c % 2, t * P:(t + 1) * P],
                                         KA[:, c * CHUNK + t * P:c * CHUNK + (t + 1) * P], ffn_w[:, 2, :],
                                         start=True, stop=True)
                    done.then_inc(s_v, 1)

                keys_gates(0)
                for c in range(1, CHUNKS):
                    keys_gates(c)
                    values(c - 1)
                values(CHUNKS - 1)

            pe.wait_ge(s_ident, 1)
            pe.wait_ge(s_bias_in, 16 * 3)
            for c in range(8):
                pe.matmul(OM[:, 1, 0:E], bv_col[:, c:c + 1].to_broadcast([P, P]), wo_all[:, c * E:(c + 1) * E],
                          start=(c == 0), stop=False)
            pe.matmul(OM[:, 1, 0:E], one_row, bo_row, start=False, stop=True).then_inc(s_bias_ps, 1)
            transpose_input(0)
            pe.wait_ge(s_small, 16 * 5)
            pe.wait_ge(s_bias, 1)
            ffn(0)
            transpose_input(1)

            def project(i, ahead, f, number):
                c, what = PROJ_ORDER[f]
                if not (isinstance(number, int) and number == 0):
                    pe.wait_ge(s_misc, number)
                pe.wait_ge(s_ws2, at(i, ahead, 4, 4))
                pe.wait_ge(s_xs2, at(i, ahead, 2, c + 1))
                for n, (w, x) in enumerate(((ws1, xs1), (ws1, xs2), (ws2, xs1))):
                    if what < 4:
                        done = pe.matmul(OM[:, 1, :], w[:, what * P:(what + 1) * P], x[:, :],
                                         start=(n == 0), stop=(n == 2))
                    else:
                        done = pe.matmul(OM[:, 1, 0:W_V], x[:, (what - 4) * P:(what - 3) * P], w[:, W_QK:],
                                         start=(n == 0), stop=(n == 2))
                done.then_inc(s_fill, 1)

            def scores(i, tile):
                ahead, u, k = tile
                h, t, place = u // 2, GROUPS[u % 2][k], (3 - k) % 2
                n = score_no(i, tile)
                if k == 3:
                    pe.wait_ge(s_stack[h], at(i, ahead, STACK_DMAS * 16, STACK_DMAS * 16))
                if not (isinstance(n, int) and n < 2):
                    pe.wait_ge(s_probs, n - 1)
                for half in range(2):
                    for c0 in range(0, (t + 1) * P, CHUNK):
                        c1 = min(c0 + CHUNK, (t + 1) * P)
                        pe.matmul(SC[:, place, c0:c1], QS[:, h, half, t * P:(t + 1) * P], KS[:, h, c0:c1],
                                  start=(half == 0), stop=(half == 1 and c1 < (t + 1) * P))
                pe.matmul(SC[:, place, t * P:(t + 1) * P], ident_bf[:, :], mask_bf[:, :],
                          start=False, stop=True).then_inc(s_scores, 1)

            def transposes(i, ahead, u, j, first):
                m, slot, col = step_no(i, ahead, u, j), (UNIT_STEPS * u + j) % 2, 0
                if j == 0:
                    pe.wait_ge(s_norm, at(i, ahead, 4 * UNITS, 4 * u + 4))
                if not first or j >= 2:
                    pe.wait_ge(s_p2, m - 1)
                for block, k0 in STEPS[u % 2][j]:
                    for k in range(k0, 4):
                        off = probs_of(u, k)[0].start + block * P
                        done = pe.transpose(TB[:, slot, col:col + P], probs[:, off:off + P], ident[:, :])
                        col += P
                done.then_inc(s_pt, 1)

            def values(i, ahead, u, j, first=False):
                h, m, slot, col = u // 2, step_no(i, ahead, u, j), (UNIT_STEPS * u + j) % 2, 0
                pe.wait_ge(s_p2, m + 1)
                if j == 0:
                    pe.wait_ge(s_vcopy[h], at(i, ahead, 16, 16))
                    if not first:
                        pe.wait_ge(s_ot, at(i, ahead, UNITS, u))
                step = STEPS[u % 2][j]
                for block, k0 in step:
                    width = (4 - k0) * P
                    for part in (p1, p2):
                        final = j == UNIT_STEPS - 1 and part is p2 and block == step[-1][0]
                        done = pe.matmul(OM[:, 0, k0 * P:], V[:, h, block, :], part[:, slot, col:col + width],
                                         start=(block == 0 and part is p1), stop=final)
                    col += width
                done.then_inc(s_av, 1)

            def project_out(i, g, number):
                pe.wait_ge(s_misc, number)
                pe.wait_ge(s_wo, at(i, 0, 32, 32))
                pe.wait_ge(s_ot, at(i, 0, UNITS, UNITS - 1 + g))
                for t in range(4):
                    for h in range(QUAD):
                        done = pe.matmul(OM[:, 1, t * P:(t + 1) * P],
                                         OT[:, h, (4 * g + t) * P:(4 * g + t + 1) * P], wo_s[:, h, :],
                                         start=(h == 0), stop=(h == QUAD - 1))
                done.then_inc(s_fill, 1)

            def pe_run(i, steps, first=False, last=False):
                for s in steps:
                    ahead, u, j = s["ahead"], s["unit"], s["j"]
                    transposes(i, ahead, u, j, first)
                    if s["score"]:
                        scores(i, s["score"])
                    for f in s["fills"]:
                        project(i, 1, f, at(i, 0, FILLS, PROJ + f))
                    for g in s["outs"]:
                        project_out(i, g, out_no(i, g, last))
                    if j:
                        values(i, ahead, u, j - 1, first)
                    elif not first:
                        values(i, ahead - (u == 0), (u - 1) % UNITS, UNIT_STEPS - 1)

            for f in range(PROJ):
                project(0, 0, f, f)
            for k in (3, 2, 1, 0):
                scores(0, (0, 0, k))
            scores(0, (0, 1, 3))
            pe_run(0, HEAD, first=True)
            with pe.Fori(0, ITERS - 1) as i:
                pe_run(i, BODY)
            pe_run(ITERS - 1, TAIL, last=True)
            values(ITERS - 1, 0, UNITS - 1, UNIT_STEPS - 1)
            project_out(ITERS - 1, 1, out_no(ITERS - 1, 1, True))

            transpose_input(2)
            ffn(1)


def rotary_tables():
    theta = np.float32(10000.0) ** (np.arange(0, DK, 2, dtype=np.float32) / np.float32(DK))
    freqs = np.arange(S, dtype=np.float32)[:, None] * (np.float32(1.0) / theta)[None, :]
    emb = np.concatenate([freqs, freqs], axis=-1).T
    even, odd = np.tile(emb[0::2], (QUAD, 1)), np.tile(emb[1::2], (QUAD, 1))
    return np.stack([np.cos(even), np.sin(odd), np.cos(odd), -np.sin(even)], axis=1).astype(np.float32)


def kernel(**inputs):
    import concourse.bacc as bacc
    from concourse.bass_utils import run_bass_kernel_spmd

    a = {k: np.asarray(v) for k, v in inputs.items()}

    def halves(w):
        w = w.reshape(QUADS, QUAD, HALF, 2, -1).transpose(0, 3, 1, 2, 4)
        return w.reshape(QUADS, 2, P, -1)

    qk = np.concatenate([halves(a["L0_attn_wq"]), halves(a["L0_attn_wk"])], axis=1)
    qk = qk.transpose(0, 3, 1, 2).reshape(QUADS, E, W_QK)
    wv = a["L0_attn_wv"].reshape(QUADS, W_V, E).transpose(0, 2, 1)
    biases = np.concatenate([halves(a["L0_attn_bq"]), halves(a["L0_attn_bk"])], axis=1)[..., 0]
    odd = np.zeros((P, CHUNKS), np.float32)
    odd[:, 1::2] = 1.0
    arrays = {
        "x": a["L0_attn_x"],
        "w_heads": np.concatenate([qk, wv], axis=2),
        "b_heads": biases.transpose(0, 2, 1),
        "wo_t": a["L0_attn_wo"].T,
        "bv": a["L0_attn_bv"].reshape(8, P).T,
        "bo": a["L0_attn_bo"].reshape(1, E),
        "rope": rotary_tables(),
        "wr_t": a["L0_ffn_W_r"].T,
        "wk_t": a["L0_ffn_W_k"].T,
        "wv_t": a["L0_ffn_W_v"].T,
        "mu": np.stack([a["L0_ffn_mu_r"], a["L0_ffn_mu_k"]], axis=1),
        "odd": odd,
    }
    arrays = {k: np.ascontiguousarray(v) for k, v in arrays.items()}
    nc = bacc.Bacc("TRN2", target_bir_lowering=False, num_devices=1)
    aps = [nc.dram_tensor("in_" + k, v.shape, F32, kind="ExternalInput").ap() for k, v in arrays.items()]
    out = nc.dram_tensor("y", (B, S, E), F32, kind="ExternalOutput").ap()
    macaron(nc, *aps, out)
    result = run_bass_kernel_spmd(nc, [{"in_" + k: v for k, v in arrays.items()}], core_ids=[0])
    return result.results[0]["y"]
```

```python
from contextlib import ExitStack

import numpy as np

import concourse.bass as bass
from concourse import mybir

ALU = mybir.AluOpType
ACT = mybir.ActivationFunctionType
F32 = mybir.dt.float32
F32R = mybir.dt.float32r
BF16 = mybir.dt.bfloat16
AX_X = mybir.AxisListType.X

P = 128
B, S, E = 2, 1024, 128
H, DK = 16, 64
TILES = B * S // P
CHUNK = 512
CHUNKS = B * S // CHUNK
PER_CHUNK = CHUNK // P
QUAD = 4
QUADS = H // QUAD
ITERS = B * QUADS
HALF = DK // 2
EPS = 1e-5
SCALE = 1.0 / 8.0
MASKED = -1e30

W_QK = 4 * P
W_V = QUAD * DK
W_ALL = W_QK + W_V

GROUPS = [(0, 3, 4, 7), (1, 2, 5, 6)]
UNITS = 2 * QUAD
STEPS = [[[(0, 0)], [(1, 1), (5, 3)], [(2, 1), (6, 3)], [(3, 1), (7, 3)], [(4, 2)]],
         [[(0, 0)], [(1, 0)], [(2, 1), (6, 3)], [(3, 2), (4, 2)], [(5, 2)]]]
UNIT_STEPS = len(STEPS[0])
ALL_STEPS = UNITS * UNIT_STEPS
GROUP_BLOCKS = sum(t + 1 for t in GROUPS[0])
P_COLS = 2 * GROUP_BLOCKS * P

PROJ = 16
FILLS = PROJ + 2
PROJ_ORDER = [(0, 0), (0, 1), (0, 4), (0, 2), (0, 3), (1, 0), (0, 5), (1, 1), (1, 2), (0, 6), (0, 7), (1, 3), (1, 4), (1, 5), (1, 6), (1, 7)]
FIRST_VALUE = min(f for f, (_, what) in enumerate(PROJ_ORDER) if what >= 4)
CHUNK0_FILLS = 1 + max(f for f, (c, _) in enumerate(PROJ_ORDER) if c == 0)
PROJ_AT = [(0, 0), (0, 3), (1, 0), (1, 3), (2, 0), (2, 2), (2, 4), (3, 0), (3, 4), (4, 1), (4, 2), (4, 3), (5, 0), (5, 3), (6, 0), (6, 3)]
OUT_AT = [(7, 2), (0, 2)]
SCORES_AT = {1: (1, (2, 1)), 2: (1, (0,)), 4: (2, (3,))}
STATISTICS_AT = {(3, 0): 0, (3, 3): 1}
SCALE_AT = {(4, 0): 0, (4, 2): 1}
NORMALIZE_AT = {(5, 0): 0, (5, 3): 1}
TRANSPOSE_AT = {(7, 1): 0, (7, 3): 1}
COPY_AT = {(7, 2): 0, (7, 4): 1}
SCORE_SETS = len(SCORES_AT)
EARLY = sum(unit == 0 for unit, _ in PROJ_AT)
K_EVAC=2
K_LATE=0
K_RECIP=0
K_FILLFIRST=0
K_PE='SFV'
ROUND = 3


FIRST_ORDER = [(c, what) for c in range(2) for what in range(4)] + \
              [(c, what) for c in range(2) for what in range(4, 8)]


def step_cols(step):
    return sum(4 - k0 for _, k0 in step) * P


def at(i, ahead, per, rest):
    return i * per + (ahead * per + rest)


def schedule(units, last):
    steps, count = [], 0
    exp = [(0, units[0] + 1, 3)]
    for n, u in enumerate(units):
        ahead = 1 if n and u == 0 else 0
        for j in range(UNIT_STEPS):
            later, tiles = SCORES_AT.get(j, (0, ()))
            score = [(ahead + (u + later) // UNITS, (u + later) % UNITS, k) for k in tiles]
            if last:
                score = [tile for tile in score if not tile[0]]
            outs = [g for g in range(2) if OUT_AT[g] == (u, j) and (n or u)]
            fills = [] if last else [f for f, place in enumerate(PROJ_AT) if place == (u, j)]
            fills, outs = [(f, count + k) for k, f in enumerate(fills)], [(g, count + len(fills)) for g in outs]
            count += len(fills) + len(outs)
            steps.append(dict(ahead=ahead, unit=u, j=j, score=score, exp=exp, fills=fills, outs=outs, round=[]))
            exp = score
    for n, s in enumerate(steps):
        for f, _ in s["fills"]:
            if PROJ_ORDER[f][1] in (1, 3) and (len(units) > 1 or n + ROUND < len(steps)):
                steps[(n + ROUND) % len(steps)]["round"].append(f)
    return steps


STACK_DMAS = 8


def fill_of(f, fixed=False):
    return (FIRST_ORDER if fixed else PROJ_ORDER)[f]


def pair_of(f, fixed=False):
    c, what = fill_of(f, fixed)
    return 2 * c + what // 2


def macaron(nc, x_in, w_heads, b_heads, wo_t, bv_in, bo_in, rope_in, wr_t, wk_t, wv_t, mu_in, out):
    ctx = ExitStack()
    with ctx:
        def sb(name, shape, dt=F32):
            return ctx.enter_context(nc.sbuf_tensor(name, shape, dt))

        def ps(name, shape):
            return ctx.enter_context(nc.psum_tensor(name, shape, F32))

        def sem(name):
            return ctx.enter_context(nc.semaphore(name))

        x_dram = nc.dram_tensor("x_scratch", (CHUNKS, P, 2 * CHUNK), F32).ap()
        w_dram = nc.dram_tensor("w_scratch", (QUADS, P, 2 * W_ALL), F32).ap()

        X = sb("X", [P, TILES, E])
        ident = sb("ident", [P, P])
        ident_bf = sb("ident_bf", [P, P], BF16)
        mask_bf = sb("mask_bf", [P, P], BF16)
        ffn_w = sb("ffn_w", [P, 5, P])
        mu = sb("mu", [P, 2])
        bn = sb("bn", [P, TILES, 6])
        mv = sb("mv", [P, TILES, 2])
        var_eps = sb("var_eps", [P, TILES])
        rstd = sb("rstd", [P, TILES])
        neg_half = sb("neg_half", [P, PER_CHUNK])
        eps = sb("eps", [P, PER_CHUNK])
        xs = sb("xs", [P, 2, 2, CHUNK], F32R)
        ws = sb("ws", [P, 2, W_ALL], F32R)
        b_all = sb("b_all", [P, QUADS, 4])
        wo_s = sb("wo_s", [P, QUAD, E])
        rope = sb("rope", [P, 4, S])
        rt = sb("rt", [P, 4, CHUNK])
        parts = sb("parts", [P, 8, S], F32R)
        QS = sb("QS", [P, QUAD, 2, S], F32R)
        KS = sb("KS", [P, QUAD, S], F32R)
        V_next = sb("V_next", [P, QUAD, 8, P], F32R)
        V = sb("V", [P, QUAD, 8, P], F32R)
        probs = sb("probs", [P, P_COLS])
        p1 = sb("p1", [P, 2, CHUNK], F32R)
        p2 = sb("p2", [P, 2, CHUNK], F32R)
        OT = sb("OT", [P, QUAD, S])
        neg_max = sb("neg_max", [P, 8])
        row_sum = sb("row_sum", [P, 8])
        recip = sb("recip", [P, 8])
        XN = rt[:, :, :].rearrange("p a b -> p (a b)")
        flat_OT = OT[:, :, :].rearrange("p a b -> p (a b)")
        flat_rope = rope[:, :, :].rearrange("p a b -> p (a b)")
        XT = [flat[:, 0:B * (S + 1)] for flat in (flat_OT, flat_rope)]
        KA = [flat[:, B * (S + 1):B * (S + 1) + 2 * CHUNK] for flat in (flat_OT, flat_rope)]
        wo_half = [flat_OT[:, 3080:3080 + 4 * E], probs[:, P_COLS - 4 * E:]]
        bv_col = flat_OT[:, 3600:3608]
        bo_row = flat_OT[0:1, 3700:3700 + E]
        one_row = flat_OT[0:1, 3900:3900 + P]
        flat_parts = parts[:, :, :].rearrange("p a n -> p (a n)")
        w_raw = flat_parts[:, 0:QUADS * W_ALL].bitcast(F32).rearrange("p (q n) -> p q n", q=QUADS)
        flat_QS = QS[:, :, :, :].rearrange("p h a n -> p (h a n)")
        w_staged = flat_QS[:, 0:2 * (QUADS - 1) * W_ALL].rearrange("p (q a n) -> p q a n", q=QUADS - 1, a=2)
        w_split = [ws[:, :, :]] + [w_staged[:, q] for q in range(QUADS - 1)]
        flat_V = V[:, :, :, :].rearrange("p h b n -> p (h b n)")
        x_split = flat_V[:, 0:4 * CHUNK].rearrange("p (c a n) -> p c a n", c=2, a=2)
        cbias = sb("cbias", [P, E])

        SC = ps("SC", [P, 2, S])
        TB = ps("TB", [P, 2, CHUNK])
        OM = ps("OM", [P, 2, CHUNK])
        SC4 = SC[:, :, :].rearrange("p a (b n) -> p (a b) n", n=CHUNK)

        s_x = [sem(f"s_x{c}") for c in range(CHUNKS)]; s_small = sem("s_small"); s_setup = sem("s_setup"); s_ident = sem("s_ident")
        s_bn = sem("s_bn"); s_mv = sem("s_mv"); s_eps = sem("s_eps"); s_rstd = sem("s_rstd")
        s_xn = sem("s_xn"); s_xnt = sem("s_xnt"); s_xt = sem("s_xt"); s_wmix = sem("s_wmix")
        s_k = sem("s_k"); s_r = sem("s_r")
        s_zero = sem("s_zero"); s_relu = sem("s_relu"); s_ka = sem("s_ka"); s_sg = sem("s_sg"); s_v = sem("s_v")
        s_half = sem("s_half"); s_ffn = sem("s_ffn")
        s_bias_in = sem("s_bias_in"); s_bias_ps = sem("s_bias_ps"); s_bias = sem("s_bias")
        s_biased = sem("s_biased")
        s_scratch_w = sem("s_scratch_w"); s_scratch_x = sem("s_scratch_x"); s_bsc = sem("s_bsc")
        s_rope_in = sem("s_rope_in"); s_out = sem("s_out")
        s_w_raw = sem("s_w_raw"); s_w = sem("s_w"); s_xs = [sem("s_xs_0"), sem("s_xs_1")]; s_wo = sem("s_wo")
        s_ws1 = sem("s_ws1"); s_ws2 = sem("s_ws2"); s_xs1 = sem("s_xs1"); s_xs2 = sem("s_xs2")
        s_fill = sem("s_fill"); s_misc = sem("s_misc")
        s_rope = sem("s_rope"); s_radd = sem("s_radd"); s_radd_odd = sem("s_radd_odd"); s_rnd = sem("s_rnd"); s_sub = sem("s_sub")
        s_v1 = sem("s_v1")
        s_stack = [sem(f"s_stack{h}") for h in range(QUAD)]
        s_vcopy = [sem(f"s_vcopy{h}") for h in range(QUAD)]
        s_scores = sem("s_scores"); s_max = sem("s_max"); s_probs = sem("s_probs")
        s_recip = sem("s_recip"); s_norm = sem("s_norm")
        s_pt = sem("s_pt"); s_p1 = sem("s_p1"); s_p2 = sem("s_p2"); s_av = sem("s_av"); s_ot = sem("s_ot")

        BODY = schedule([1, 2, 3, 4, 5, 6, 7, 0], False)
        HEAD = schedule([0], False)
        TAIL = schedule([1, 2, 3, 4, 5, 6, 7], True)

        def fill_no(i, k, first=False):
            return PROJ + k if first else at(i, 0, FILLS, PROJ + EARLY + k)

        FILL_K = {f: k for s in BODY for f, k in s["fills"]}
        OUT_K = {g: k for s in BODY for g, k in s["outs"]}

        def score_no(i, tile):
            ahead, u, k = tile
            return at(i, ahead, 4 * UNITS, 4 * u + 3 - k)

        def scores_of(u, k):
            place = (SCORE_SETS * u + min(3 - k, 2)) % 2
            start = CHUNK if k == 0 else 0
            return SC[:, place, start:start + (GROUPS[u % 2][k] + 1) * P]

        def step_no(i, ahead, u, j):
            return at(i, ahead, ALL_STEPS, UNIT_STEPS * u + j)

        def probs_of(u, k):
            group = GROUPS[u % 2]
            start = ((u % 2) * GROUP_BLOCKS + sum(t + 1 for t in group[:k])) * P
            return slice(start, start + (group[k] + 1) * P), group[k]

        FFN_K, FFN_K_PREV, FFN_R, FFN_R_PREV, FFN_V = range(5)

        def xt_of(f, c, shift):
            start = (c // 2) * (S + 1) + (c % 2) * CHUNK + 1 - shift
            return XT[f][:, start:start + CHUNK]

        def rotation(pair, fixed):
            if fixed and pair in (1, 2):
                return probs[:, (pair - 1) * 4 * CHUNK:pair * 4 * CHUNK].rearrange("p (a n) -> p a n", a=4)
            return rt[:, :, :]

        def spare(f, fixed):
            return SC4[:, f % 4, :] if fixed else OM[:, 1, :]

        block = ctx.enter_context(nc.Block())


        @block.sync
        def _(sp):
            x_view = x_in.rearrange("b (t p) e -> p (b t) e", p=P)
            for c in range(CHUNKS):
                sp.dma_start(X[:, 4 * c:4 * c + 4, :], x_view[:, 4 * c:4 * c + 4, :]).then_inc(s_x[c], 16)
                if c == 1:
                    for place, source in ((FFN_K_PREV, wk_t), (FFN_R_PREV, wr_t), (FFN_V, wv_t)):
                        sp.dma_start(ffn_w[:, place, :], source).then_inc(s_small, 16)
                    sp.dma_start(mu[:, :], mu_in).then_inc(s_small, 16)
            sp.dma_start(w_raw, w_heads.rearrange("q p n -> p q n")).then_inc(s_w_raw, 16)
            sp.dma_start(b_all[:, :, :], b_heads.rearrange("q p n -> p q n")).then_inc(s_w_raw, 16)

            for half in range(2):
                sp.dma_start(wo_half[half].rearrange("p (c e) -> p c e", e=E),
                             wo_t.rearrange("(a c p) e -> a p c e", a=2, p=P)[half]).then_inc(s_bias_in, 16)
            sp.dma_start(bv_col, bv_in).then_inc(s_bias_in, 16)
            sp.dma_start(bo_row, bo_in).then_inc(s_bias_in, 16)

            sp.dma_start(rope[:, :, :], rope_in).then_inc(s_rope_in, 16)

            def load_weights(i):
                sp.dma_start(ws[:, :, :].rearrange("p a n -> p (a n)").bitcast(F32),
                             w_dram[bass.ds(i % QUADS, 1)].rearrange("a p n -> (a p) n")).then_inc(s_w, 16)

            def load_x(i, c):
                sp.dma_start(xs[:, c, :, :].rearrange("p a n -> p (a n)").bitcast(F32),
                             x_dram[bass.ds(2 * ((i % ITERS) // QUADS) + c, 1)]
                             .rearrange("a p n -> (a p) n")).then_inc(s_xs[c], 16)

            def load_wo(i):
                for r in range(2):
                    sp.dma_start(wo_s[r * DK:(r + 1) * DK, :, :],
                                 wo_t.rearrange("(q h d) e -> q d h e", q=QUADS, h=QUAD)
                                 [bass.ds(i % QUADS, 1)].rearrange("a d h e -> (a d) h e")).then_inc(s_wo, 16)

            def stack_queries(h):
                rows = slice(HALF * h, HALF * (h + 1))
                for strip, part in enumerate((0, 1, 0, 1)):
                    sp.dma_start(QS[HALF * strip:HALF * (strip + 1), h, :, :].bitcast(F32),
                                 parts[rows, part:part + 3:2, :].bitcast(F32)).then_inc(s_stack[h], 16)

            def stack_keys(h):
                rows = slice(HALF * h, HALF * (h + 1))
                for strip in range(4):
                    sp.dma_start(KS[HALF * strip:HALF * (strip + 1), h, :].bitcast(F32),
                                 parts[rows, 4 + strip, :].bitcast(F32)).then_inc(s_stack[h], 16)

            def copy_values(i, h):
                sp.wait_ge(s_av, i * ALL_STEPS + 2 * UNIT_STEPS * (h + 1))
                sp.nop(nofuse=True)
                sp.dma_start(V[:, h, :, :].bitcast(F32), V_next[:, h, :, :].bitcast(F32)).then_inc(s_vcopy[h], 16)

            for q in range(QUADS):
                sp.wait_ge(s_ws2, 2 * q + 2)
                sp.dma_start(w_dram[q], w_split[q].rearrange("p a n -> p (a n)").bitcast(F32)
                             ).then_inc(s_scratch_w, 16)
            for c in range(CHUNKS):
                sp.wait_ge(s_xs2, c + 1)
                source = xs[:, c, :, :] if c < 2 else x_split[:, c - 2, :, :]
                sp.dma_start(x_dram[c], source.rearrange("p a n -> p (a n)").bitcast(F32)).then_inc(s_scratch_x, 16)
            sp.wait_ge(s_scratch_w, 16 * QUADS)
            sp.wait_ge(s_scratch_x, 16 * CHUNKS)
            sp.wait_ge(s_sub, 6)
            stack_queries(0)
            sp.wait_ge(s_sub, 8)
            stack_keys(0)
            sp.wait_ge(s_misc, PROJ)
            for h in range(QUAD):
                if h == 1:
                    load_weights(1)
                    for c in range(2):
                        load_x(1, c)
                if h:
                    stack_queries(h)
                    stack_keys(h)
                sp.dma_start(V[:, h, :, :].bitcast(F32), V_next[:, h, :, :].bitcast(F32)).then_inc(s_vcopy[h], 16)

            with sp.Fori(0, ITERS - 1) as i:
                sp.wait_ge(s_fill, fill_no(i, OUT_K[1] - FILLS + 1))
                sp.nop(nofuse=True)
                load_wo(i)
                sp.wait_ge(s_fill, fill_no(i, FILL_K[CHUNK0_FILLS - 1] + 1))
                sp.nop(nofuse=True)
                load_x(i + 2, 0)
                for h in range(QUAD):
                    if h == 0:
                        sp.wait_ge(s_sub, i * 8 + 14)
                        sp.nop(nofuse=True)
                    if h == QUAD - 1:
                        sp.wait_ge(s_misc, fill_no(i, FILL_K[PROJ - 1] + 1))
                        sp.nop(nofuse=True)
                        for done in range(QUAD - 1):
                            copy_values(i, done)
                        sp.wait_ge(s_fill, fill_no(i, FILL_K[PROJ - 1] + 1))
                        sp.nop(nofuse=True)
                        load_weights(i + 2)
                        load_x(i + 2, 1)
                    sp.wait_ge(s_scores, i * 32 + 8 * h + 8)
                    sp.nop(nofuse=True)
                    stack_queries(h)
                    if h == 0:
                        sp.wait_ge(s_sub, i * 8 + 16)
                        sp.nop(nofuse=True)
                    stack_keys(h)
                copy_values(i, QUAD - 1)
            sp.wait_ge(s_fill, fill_no(ITERS - 1, OUT_K[1] - FILLS + 1))
            load_wo(ITERS - 1)
            out_view = out.rearrange("b (t p) e -> p (b t) e", p=P)
            for c in range(CHUNKS):
                sp.wait_ge(s_ffn, CHUNKS + c + 1)
                sp.dma_start(out_view[:, 4 * c:4 * c + 4, :], X[:, 4 * c:4 * c + 4, :]).then_inc(s_out, 16)
            sp.wait_ge(s_out, 16 * CHUNKS)

        @block.gpsimd
        def _(pool):
            pool.memset(ident[:, :], 0.0).then_inc(s_setup, 1)
            pool.memset(mask_bf[:, :], 0.0).then_inc(s_setup, 1)
            pool.memset(neg_half[:, :], -0.5).then_inc(s_setup, 1)
            pool.memset(eps[:, :], EPS).then_inc(s_setup, 1)
            pool.memset(one_row, 1.0).then_inc(s_setup, 1)
            pool.memset(XT[0][:, 0:1], 0.0).then_inc(s_zero, 1)
            pool.memset(XT[0][:, S + 1:S + 2], 0.0).then_inc(s_zero, 1)
            pool.wait_ge(s_setup, 5)
            pool.affine_select(out=ident[:, :], in_=ident[:, :], compare_op=ALU.not_equal, fill=1.0, base=0,
                               pattern=[[-1, P]], channel_multiplier=1).then_inc(s_setup, 1)
            pool.affine_select(out=mask_bf[:, :], in_=mask_bf[:, :], compare_op=ALU.is_ge, fill=MASKED, base=0,
                               pattern=[[-1, P]], channel_multiplier=1).then_inc(s_setup, 1)
            pool.wait_ge(s_setup, 7)
            pool.tensor_copy(ident_bf[:, :], ident[:, :]).then_inc(s_ident, 1)

            def norm_scale(n, chunks=range(CHUNKS)):
                for c in chunks:
                    pool.wait_ge(s_mv, 16 * n + 4 * c + 4)
                    tiles = slice(4 * c, 4 * c + 4)
                    pool.tensor_tensor(var_eps[:, tiles], mv[:, tiles, 1], eps[:, :], ALU.add).then_inc(s_eps, 1)
                    pool.wait_ge(s_eps, 4 * n + c + 1)
                    pool.tensor_tensor(rstd[:, tiles], var_eps[:, tiles], neg_half[:, :], ALU.pow).then_inc(s_rstd, 1)

            norm_scale(0)
            norm_scale(1)
            def rotate_add(i, ahead, f, number):
                a = pair_of(f) % 2
                pool.wait_ge(s_rope, at(i, ahead, 8, 2 * pair_of(f) + 2))
                pool.wait_ge(s_misc, number + 1)
                pool.tensor_tensor(rt[:, a, :], rt[:, a, :], rt[:, 1 - a, :], ALU.add).then_inc(s_radd, 1)
                pool.tensor_tensor(rt[:, 2 + a, :], rt[:, 2 + a, :], rt[:, 3 - a, :], ALU.add).then_inc(s_radd, 1)

            def rotate_add_even(f):
                a, places = pair_of(f, True) % 2, rotation(pair_of(f, True), True)
                pool.wait_ge(s_rope, 2 * pair_of(f, True) + 2)
                pool.wait_ge(s_misc, f + 1)
                pool.tensor_tensor(places[:, a, :], places[:, a, :], places[:, 1 - a, :], ALU.add).then_inc(s_radd, 2)

            def rotate_rest(i, ahead, f, fixed=False):
                c, what = fill_of(f, fixed)
                base, cols = 4 * (what // 2), slice(c * CHUNK, (c + 1) * CHUNK)
                pool.wait_ge(s_rnd, at(i, ahead, 8, 2 * pair_of(f, fixed) + 2))
                for half in range(2):
                    pool.tensor_tensor(parts[:, base + 2 + half, cols], rotation(pair_of(f, fixed), fixed)[:, 2 * half + pair_of(f, fixed) % 2, :],
                                       parts[:, base + half, cols].bitcast(F32), ALU.subtract).then_inc(s_sub, 1)

            def normalize(i, tile):
                cols, slot = probs_of(*tile[1:])
                pool.wait_ge(s_recip, score_no(i, tile) + 1)
                pool.nop(nofuse=True)
                pool.tensor_scalar(probs[:, cols], probs[:, cols], recip[:, slot:slot + 1], 1.0,
                                   ALU.mult, ALU.mult).then_inc(s_norm, 1)

            def pool_run(i, steps, first=False, last=False):
                for s in steps:
                    if last and (s["unit"], s["j"]) in SCALE_AT:
                        norm_scale(2, (SCALE_AT[s["unit"], s["j"]],))
                    for tile in s["exp"]:
                        normalize(i, tile)
                    for f, k in s["fills"]:
                        if PROJ_ORDER[f][1] in (1, 3):
                            rotate_add(i, s["ahead"] + 1, f, fill_no(i, k, first))
                    for f in s["round"]:
                        rotate_rest(i, s["ahead"] + 1, f)

            for f in range(PROJ):
                if FIRST_ORDER[f][1] in (1, 3):
                    rotate_add_even(f)
                    rotate_rest(0, 0, f, fixed=True)
            for k in (3, 2, 1, 0):
                normalize(0, (0, 0, k))
            pool_run(0, HEAD, first=True)
            with pool.Fori(0, ITERS - 1) as i:
                pool_run(i, BODY)
            pool.memset(XT[1][:, 0:1], 0.0).then_inc(s_zero, 1)
            pool.memset(XT[1][:, S + 1:S + 2], 0.0).then_inc(s_zero, 1)
            pool_run(ITERS - 1, TAIL, last=True)
            norm_scale(2, (2, 3))

        @block.scalar
        def _(act):
            def transposed(n, f, c):
                act.wait_ge(s_xnt, 4 * n + c + 1)
                act.activation(xt_of(f, c, 0), SC4[:, c, :], ACT.Copy).then_inc(s_xt, 1)

            def relu(f, c):
                act.wait_ge(s_k, 4 * f + c + 1)
                if c >= 2:
                    act.wait_ge(s_v, 4 * f + c - 1)
                act.activation(KA[f][:, (c % 2) * CHUNK:(c % 2 + 1) * CHUNK], TB[:, c % 2, :], ACT.Relu
                               ).then_inc(s_relu, 1)

            def gate(f, c):
                act.wait_ge(s_r, 4 * f + c + 1)
                act.activation(XN[:, c * CHUNK:(c + 1) * CHUNK], SC4[:, c, :], ACT.Sigmoid).then_inc(s_sg, 1)

            def split_weights(q):
                if q == 0:
                    act.wait_ge(s_w_raw, 32)
                act.activation(w_split[q][:, 0, 0:2 * P], w_raw[:, q, 0:2 * P], ACT.Copy, scale=SCALE
                               ).then_inc(s_ws1, 1)
                act.activation(w_split[q][:, 0, 2 * P:], w_raw[:, q, 2 * P:], ACT.Copy).then_inc(s_ws1, 1)

            def split_x(c):
                act.wait_ge(s_xnt, 4 + c + 1)
                target = xs[:, c, 0, :] if c < 2 else x_split[:, c - 2, 0, :]
                act.activation(target, SC4[:, c, :], ACT.Copy).then_inc(s_xs1, 1)

            def ffn_gates(f, n):
                if f == 0:
                    transposed(n, f, 0)
                    transposed(n, f, 1)
                for c in range(CHUNKS):
                    if f == 0:
                        split_weights(c)
                    relu(f, c)
                    gate(f, c)
                    if f == 0 and c + 2 < CHUNKS:
                        transposed(n, f, c + 2)
                    if f == 1 and c == 1:
                        transposed(n, f, 2)
                        transposed(n, f, 3)

            ffn_gates(0, 0)
            for c in range(CHUNKS):
                split_x(c)

            def value_head(i, ahead, f, number, fixed=False):
                c, what = fill_of(f, fixed)
                act.wait_ge(s_fill, number + 1)
                act.activation(V_next[:, :, 4 * c + what - 4, 0:DK],
                               spare(f, fixed)[:, 0:W_V].rearrange("p (h d) -> p h d", h=QUAD), ACT.Copy).then_inc(s_v1, 1)

            def rotate_round(i, ahead, f, fixed=False):
                c, what = fill_of(f, fixed)
                for half in range(2):
                    if fixed:
                        act.wait_ge(s_radd_odd if half else s_radd, (pair_of(f, True) + 1) * (2 - half))
                    else:
                        act.wait_ge(s_radd, at(i, ahead, 8, 2 * pair_of(f) + half + 1))
                    act.activation(parts[:, 4 * (what // 2) + half, c * CHUNK:(c + 1) * CHUNK],
                                   rotation(pair_of(f, fixed), fixed)[:, 2 * half + pair_of(f, fixed) % 2, :], ACT.Copy).then_inc(s_rnd, 1)

            def exponentials(i, tile):
                cols, slot = probs_of(*tile[1:])
                n = score_no(i, tile)
                act.wait_ge(s_max, n + 1)
                act.activation(probs[:, cols], scores_of(*tile[1:]), ACT.Exp,
                               bias=neg_max[:, slot:slot + 1], accum_out=row_sum[:, slot:slot + 1]
                               ).then_inc(s_probs, 1)

            def act_run(i, steps, first=False, last=False):
                for s in steps:
                    ahead, u, j = s["ahead"], s["unit"], s["j"]
                    m = step_no(i, ahead, u, j)
                    slot, cols = (UNIT_STEPS * u + j) % 2, slice(0, step_cols(STEPS[u % 2][j]))
                    if last and (u, j) in COPY_AT:
                        transposed(2, 1, COPY_AT[u, j])
                    if j == 1 and K_EVAC == 2 and not (first and u == 0):
                        evacuate(i, ahead, u)
                    act.wait_ge(s_pt, m + 1)
                    if not first or j >= 2:
                        act.wait_ge(s_av, m - 1)
                    act.activation(p1[:, slot, cols], TB[:, slot, cols], ACT.Copy).then_inc(s_p1, 1)
                    if j == 0 and K_EVAC == 1 and not first:
                        evacuate(i, ahead, u)
                    for tile in s["exp"]:
                        exponentials(i, tile)
                    if j == 0 and K_EVAC == 0 and not first:
                        evacuate(i, ahead, u)
                    for f, k in s["fills"]:
                        if f == FIRST_VALUE:
                            for h in range(QUAD):
                                act.wait_ge(s_vcopy[h], at(i, 0, 16, 16))
                        if PROJ_ORDER[f][1] >= 4:
                            value_head(i, 1, f, fill_no(i, k))
                    for f in [] if last else s["round"]:
                        if f == 1:
                            for h in range(QUAD):
                                act.wait_ge(s_stack[h], at(i, ahead, STACK_DMAS * 16, STACK_DMAS * 16))
                        rotate_round(i, ahead + 1, f)

            def evacuate(i, ahead, u):
                h, g = ((u - 1) % UNITS) // 2, (u - 1) % 2
                act.wait_ge(s_av, step_no(i, ahead, u, 0))
                act.activation(OT[:, h, g * CHUNK:(g + 1) * CHUNK], OM[:, 0, :], ACT.Copy).then_inc(s_ot, 1)

            for f in range(PROJ):
                if FIRST_ORDER[f][1] >= 4:
                    value_head(0, 0, f, f, fixed=True)
                if FIRST_ORDER[f][1] in (1, 3):
                    rotate_round(0, 0, f, fixed=True)
            for k in (3, 2, 1, 0):
                exponentials(0, (0, 0, k))
            act_run(0, HEAD, first=True)
            with act.Fori(0, ITERS - 1) as i:
                act_run(i, BODY)
            act_run(ITERS - 1, TAIL, last=True)
            evacuate(ITERS - 1, 1, 0)

            ffn_gates(1, 2)

        @block.vector
        def _(dve):
            def statistics(n, c):
                for t in range(4 * c, 4 * c + 4):
                    dve.bn_stats(bn[:, t, :], X[:, t, :]).then_inc(s_bn, 1)
                for t in range(4 * c, 4 * c + 4):
                    dve.wait_ge(s_bn, TILES * n + t + 1)
                    dve.bn_aggr(mv[:, t, :], bn[:, t, :]).then_inc(s_mv, 1)

            def normalized(n, c):
                dve.wait_ge(s_rstd, 4 * n + c + 1)
                for t in range(4 * c, 4 * c + 4):
                    dve.tensor_scalar(XN[:, t * E:(t + 1) * E], X[:, t, :], mv[:, t, 0:1], rstd[:, t:t + 1],
                                      ALU.subtract, ALU.mult).then_inc(s_xn, 1)

            def mix_weights():
                dve.wait_ge(s_small, 16 * 4)
                for n, (place, m) in enumerate(((FFN_K, 1), (FFN_R, 0))):
                    dve.tensor_scalar(ffn_w[:, place, :], ffn_w[:, place + 1, :], mu[:, m:m + 1], None,
                                      ALU.mult).then_inc(s_wmix, 1)
                for n, place in enumerate((FFN_K, FFN_R)):
                    dve.wait_ge(s_wmix, n + 1)
                    dve.tensor_tensor(ffn_w[:, place + 1, :], ffn_w[:, place + 1, :], ffn_w[:, place, :],
                                      ALU.subtract).then_inc(s_wmix, 1)

            def keys(f, c):
                dve.wait_ge(s_relu, 4 * f + c + 1)
                place = KA[f][:, (c % 2) * CHUNK:(c % 2 + 1) * CHUNK]
                dve.tensor_tensor(place, TB[:, c % 2, :], place, ALU.mult).then_inc(s_ka, 1)

            def combine(f, c):
                dve.wait_ge(s_v, 4 * f + c + 1)
                dve.wait_ge(s_sg, 4 * f + c + 1)
                gate = XN[:, c * CHUNK:(c + 1) * CHUNK]
                dve.scalar_tensor_tensor(out=gate, in0=OM[:, c % 2, :], scalar=0.5, in1=gate,
                                         op0=ALU.mult, op1=ALU.mult).then_inc(s_half, 1)
                dve.wait_ge(s_half, 4 * f + c + 1)
                x = X[:, c * 4:c * 4 + 4, :].rearrange("p t e -> p (t e)")
                dve.tensor_tensor(x, x, gate, ALU.add).then_inc(s_ffn, 1)

            def split_weights(q):
                dve.wait_ge(s_ws1, 2 * q + 1)
                dve.scalar_tensor_tensor(out=w_split[q][:, 1, 0:2 * P], in0=w_raw[:, q, 0:2 * P], scalar=SCALE,
                                         in1=w_split[q][:, 0, 0:2 * P].bitcast(F32), op0=ALU.mult,
                                         op1=ALU.subtract).then_inc(s_ws2, 1)
                dve.wait_ge(s_ws1, 2 * q + 2)
                dve.tensor_tensor(w_split[q][:, 1, 2 * P:], w_raw[:, q, 2 * P:],
                                  w_split[q][:, 0, 2 * P:].bitcast(F32), ALU.subtract).then_inc(s_ws2, 1)

            def split_x(c):
                dve.wait_ge(s_xs1, c + 1)
                chunk = xs[:, c] if c < 2 else x_split[:, c - 2]
                dve.tensor_tensor(chunk[:, 1, :], SC4[:, c, :], chunk[:, 0, :].bitcast(F32),
                                  ALU.subtract).then_inc(s_xs2, 1)

            for c in range(CHUNKS):
                dve.wait_ge(s_x[c], 16)
                statistics(0, c)
                if c:
                    normalized(0, c - 1)
                if c == 1:
                    mix_weights()
            normalized(0, CHUNKS - 1)
            dve.wait_ge(s_w_raw, 32)
            dve.tensor_scalar(b_all[:, :, 0:2], b_all[:, :, 0:2], SCALE, None, ALU.mult).then_inc(s_bsc, 1)
            keys(0, 0)
            for c in range(CHUNKS):
                if c + 1 < CHUNKS:
                    keys(0, c + 1)
                split_weights(c)
                combine(0, c)
                dve.wait_ge(s_ffn, c + 1)
                statistics(1, c)
                if c:
                    normalized(1, c - 1)
            normalized(1, CHUNKS - 1)
            for c in range(CHUNKS):
                split_x(c)

            def rotate(i, ahead, f, number, fixed=False):
                c, what = fill_of(f, fixed)
                cols = slice(c * CHUNK, (c + 1) * CHUNK)
                dve.wait_ge(s_fill, number + 1)
                a, odd_half = pair_of(f, fixed) % 2, what % 2
                if fixed and pair_of(f, fixed) == 3:
                    dve.wait_ge(s_sub, 2)
                elif not fixed:
                    dve.wait_ge(s_sub if odd_half else s_radd, at(i, ahead, 8, 2 * pair_of(f, fixed)))
                places = (3 - a, 1 - a) if odd_half else (a, 2 + a)
                bias = b_all[:, bass.ds((i + ahead) % QUADS, 1), what]if not fixed \
                    else b_all[:, 0, what:what + 1]
                for table in (0, 1):
                    product = dve.scalar_tensor_tensor(
                        out=rotation(pair_of(f, fixed), fixed)[:, places[table], :], in0=spare(f, fixed), scalar=bias,
                        in1=rope[:, [[0, 1], [2, 3]][what % 2][table], cols], op0=ALU.add, op1=ALU.mult)
                    product.then_inc(s_rope if table == 0 else s_misc, 1)

            def rotate_add_odd(f):
                a, places = pair_of(f, True) % 2, rotation(pair_of(f, True), True)
                dve.wait_ge(s_rope, 2 * pair_of(f, True) + 2)
                dve.wait_ge(s_misc, f + 1)
                dve.tensor_tensor(places[:, 2 + a, :], places[:, 2 + a, :], places[:, 3 - a, :],
                                  ALU.add).then_inc(s_radd_odd, 1)

            def value_rest(i, ahead, f, number, fixed=False):
                c, what = fill_of(f, fixed)
                dve.wait_ge(s_v1, at(i, ahead, 8, 4 * c + what - 4 + 1))
                dve.tensor_tensor(V_next[:, :, 4 * c + what - 4, DK:P],
                                  spare(f, fixed)[:, 0:W_V].rearrange("p (h d) -> p h d", h=QUAD),
                                  V_next[:, :, 4 * c + what - 4, 0:DK].bitcast(F32),
                                  ALU.subtract).then_inc(s_misc, 1)

            def maximum(i, tile):
                slot = probs_of(*tile[1:])[1]
                dve.wait_ge(s_scores, score_no(i, tile) + 1)
                dve.tensor_reduce(neg_max[:, slot:slot + 1], scores_of(*tile[1:]), AX_X, ALU.max,
                                  negate=True).then_inc(s_max, 1)

            def reciprocal(i, tile):
                slot = probs_of(*tile[1:])[1]
                dve.wait_ge(s_probs, score_no(i, tile) + 1)
                dve.reciprocal(recip[:, slot:slot + 1], row_sum[:, slot:slot + 1]).then_inc(s_recip, 1)

            def add_output(i, g, number):
                tiles = X[:, :, :].rearrange("p (b a t) e -> p b a t e", b=B, t=4)[:, bass.ds(i // QUADS, 1)]
                x = tiles.rearrange("p b a t e -> p (b a) t e")[:, :, slice(0, 4, 3) if g == 0 else slice(1, 3), :]
                dve.wait_ge(s_fill, number + 1)
                dve.tensor_tensor(x, OM[:, 1, :].rearrange("p (a t e) -> p a t e", a=2, t=2), x,
                                  ALU.add).then_inc(s_misc, 1)

            def dve_run(i, steps, first=False, last=False):
                for s in steps:
                    ahead, u, j = s["ahead"], s["unit"], s["j"]
                    m = step_no(i, ahead, u, j)
                    slot, cols = (UNIT_STEPS * u + j) % 2, slice(0, step_cols(STEPS[u % 2][j]))
                    if last and (u, j) in STATISTICS_AT:
                        dve.wait_ge(s_misc, fill_no(ITERS - 1, 0))
                        statistics(2, STATISTICS_AT[u, j])
                    if last and (u, j) in NORMALIZE_AT:
                        dve.wait_ge(s_norm, score_no(ITERS - 1, (0, 2, 3)) + 1)
                        normalized(2, NORMALIZE_AT[u, j])
                    dve.wait_ge(s_p1, m + 1)
                    if not first or j >= 2:
                        dve.wait_ge(s_av, m - 1)
                    dve.tensor_tensor(p2[:, slot, cols], TB[:, slot, cols], p1[:, slot, cols].bitcast(F32),
                                      ALU.subtract).then_inc(s_p2, 1)
                    if K_RECIP:
                        for tile in s["exp"]:
                            reciprocal(i, tile)
                    if not K_FILLFIRST:
                        for tile in s["score"]:
                            maximum(i, tile)
                    if not K_RECIP:
                        for tile in s["exp"]:
                            reciprocal(i, tile)
                    for f, k in s["fills"]:
                        number = fill_no(i, k, first)
                        (rotate if PROJ_ORDER[f][1] < 4 else value_rest)(i, ahead + 1, f, number)
                    for g, k in s["outs"]:
                        add_output(i, g, fill_no(i, k))
                    if K_FILLFIRST:
                        for tile in s["score"]:
                            maximum(i, tile)

            dve.wait_ge(s_rope_in, 16)
            dve.wait_ge(s_bsc, 1)
            for f in range(PROJ):
                (rotate if FIRST_ORDER[f][1] < 4 else value_rest)(0, 0, f, f, fixed=True)
                if FIRST_ORDER[f][1] in (1, 3):
                    rotate_add_odd(f)
            dve.wait_ge(s_bias_ps, 1)
            dve.tensor_copy(cbias[:, :], OM[:, 1, 0:E]).then_inc(s_bias, 1)
            dve.wait_ge(s_bias, 1)
            dve.wait_ge(s_xn, 2 * TILES)
            for c in range(CHUNKS):
                x = X[:, 4 * c:4 * c + 4, :]
                dve.tensor_tensor(x, x, cbias[:, :].unsqueeze(1).to_broadcast([P, 4, E]), ALU.add).then_inc(s_biased, 1)
            for k in (3, 2, 1, 0):
                maximum(0, (0, 0, k))
                reciprocal(0, (0, 0, k))
            maximum(0, (0, 1, 3))
            dve_run(0, HEAD, first=True)
            dve.wait_ge(s_biased, CHUNKS)
            with dve.Fori(0, ITERS - 1) as i:
                dve_run(i, BODY)
            dve_run(ITERS - 1, TAIL, last=True)
            add_output(ITERS - 1, 1, fill_no(ITERS - 1, 1))

            dve.wait_ge(s_misc, fill_no(ITERS - 1, 2))
            statistics(2, 2)
            statistics(2, 3)
            normalized(2, 2)
            normalized(2, 3)
            keys(1, 0)
            for c in range(CHUNKS):
                if c + 1 < CHUNKS:
                    keys(1, c + 1)
                combine(1, c)

        @block.tensor
        def _(pe):
            def transpose_input(n, c):
                if n == 1:
                    pe.wait_ge(s_sg, c + 1)
                if n == 2:
                    pe.wait_ge(s_probs, 4 * UNITS * ITERS)
                pe.wait_ge(s_xn, TILES * n + 4 * c + 4)
                for t in range(PER_CHUNK):
                    start = c * CHUNK + t * P
                    done = pe.transpose(SC4[:, c, t * P:(t + 1) * P], XN[:, start:start + P], ident[:, :])
                done.then_inc(s_xnt, 1)

            def keys_gates(f, c):
                pe.wait_ge(s_xt, 4 * f + c + 1)
                if c >= 2:
                    pe.wait_ge(s_ka, 4 * f + c - 1)
                pe.matmul(TB[:, c % 2, :], ffn_w[:, FFN_K, :], xt_of(f, c, 0), start=True, stop=False)
                pe.matmul(TB[:, c % 2, :], ffn_w[:, FFN_K_PREV, :], xt_of(f, c, 1), start=False, stop=True
                          ).then_inc(s_k, 1)
                for t in range(PER_CHUNK):
                    tile = slice(t * P, (t + 1) * P)
                    pe.matmul(SC4[:, c, tile], xt_of(f, c, 0)[:, tile], ffn_w[:, FFN_R, :], start=True, stop=False)
                    done = pe.matmul(SC4[:, c, tile], xt_of(f, c, 1)[:, tile], ffn_w[:, FFN_R_PREV, :],
                                     start=False, stop=True)
                done.then_inc(s_r, 1)

            def ffn_values(f, c):
                pe.wait_ge(s_ka, 4 * f + c + 1)
                if c >= 2:
                    pe.wait_ge(s_half, 4 * f + c - 1)
                for t in range(PER_CHUNK):
                    start = (c % 2) * CHUNK + t * P
                    done = pe.matmul(OM[:, c % 2, t * P:(t + 1) * P], KA[f][:, start:start + P],
                                     ffn_w[:, FFN_V, :], start=True, stop=True)
                done.then_inc(s_v, 1)

            pe.wait_ge(s_ident, 1)
            transpose_input(0, 0)
            pe.wait_ge(s_wmix, 4)
            pe.wait_ge(s_zero, 2)
            for c in range(CHUNKS):
                if c + 1 < CHUNKS:
                    transpose_input(0, c + 1)
                keys_gates(0, c)
                if c:
                    ffn_values(0, c - 1)
            ffn_values(0, CHUNKS - 1)
            for c in range(CHUNKS):
                transpose_input(1, c)

            def project(i, ahead, f, number, fixed=False):
                c, what = fill_of(f, fixed)
                if not fixed:
                    pe.wait_ge(s_misc, number)
                    pe.wait_ge(s_xs[c], at(i, ahead - 1, 16, 16))
                    pe.wait_ge(s_w, at(i, ahead - 1, 16, 16))
                else:
                    if f >= 4:
                        pe.wait_ge(s_misc, f - 3)
                    pe.wait_ge(s_xs2, CHUNKS)
                    pe.wait_ge(s_ws2, 2)
                for n, (a, b) in enumerate(((0, 0), (0, 1), (1, 0))):
                    w, x = ws[:, a, :], xs[:, c, b, :]
                    if what < 4:
                        done = pe.matmul(spare(f, fixed), w[:, what * P:(what + 1) * P], x,
                                         start=(n == 0), stop=(n == 2))
                    else:
                        done = pe.matmul(spare(f, fixed)[:, 0:W_V], x[:, (what - 4) * P:(what - 3) * P], w[:, W_QK:],
                                         start=(n == 0), stop=(n == 2))
                done.then_inc(s_fill, 1)

            def scores(i, tile):
                ahead, u, k = tile
                h, t, place = u // 2, GROUPS[u % 2][k], scores_of(u, k)
                n = score_no(i, tile)
                if k == 3:
                    pe.wait_ge(s_stack[h], at(i, ahead, STACK_DMAS * 16, STACK_DMAS * 16))
                if k and not (isinstance(n, int) and n < 2):
                    pe.wait_ge(s_probs, n - (2 if k == 3 else 1))
                for half in range(2):
                    for c0 in range(0, (t + 1) * P, CHUNK):
                        c1 = min(c0 + CHUNK, (t + 1) * P)
                        pe.matmul(place[:, c0:c1], QS[:, h, half, t * P:(t + 1) * P], KS[:, h, c0:c1],
                                  start=(half == 0), stop=(half == 1 and c1 < (t + 1) * P))
                pe.matmul(place[:, t * P:(t + 1) * P], ident_bf[:, :], mask_bf[:, :],
                          start=False, stop=True).then_inc(s_scores, 1)

            def transposes(i, ahead, u, j, first):
                m, slot, col = step_no(i, ahead, u, j), (UNIT_STEPS * u + j) % 2, 0
                if j == 0:
                    pe.wait_ge(s_norm, at(i, ahead, 4 * UNITS, 4 * u + 4))
                if not first or j >= 2:
                    pe.wait_ge(s_p2, m - 1)
                for block, k0 in STEPS[u % 2][j]:
                    for k in range(k0, 4):
                        off = probs_of(u, k)[0].start + block * P
                        done = pe.transpose(TB[:, slot, col:col + P], probs[:, off:off + P], ident[:, :])
                        col += P
                done.then_inc(s_pt, 1)

            def values(i, ahead, u, j, first=False):
                h, m, slot, col = u // 2, step_no(i, ahead, u, j), (UNIT_STEPS * u + j) % 2, 0
                pe.wait_ge(s_p2, m + 1)
                if j == 0:
                    pe.wait_ge(s_vcopy[h], at(i, ahead, 16, 16))
                    if not first:
                        pe.wait_ge(s_ot, at(i, ahead, UNITS, u))
                step = STEPS[u % 2][j]
                for block, k0 in step:
                    width = (4 - k0) * P
                    for part in (p1, p2):
                        final = j == UNIT_STEPS - 1 and part is p2 and block == step[-1][0]
                        done = pe.matmul(OM[:, 0, k0 * P:], V[:, h, block, :], part[:, slot, col:col + width],
                                         start=(block == 0 and part is p1), stop=final)
                    col += width
                done.then_inc(s_av, 1)

            def project_out(i, g, number):
                pe.wait_ge(s_misc, number)
                pe.wait_ge(s_wo, at(i, 0, 32, 32))
                pe.wait_ge(s_ot, at(i, 0, UNITS, UNITS - 1 + g))
                for t in range(4):
                    for h in range(QUAD):
                        done = pe.matmul(OM[:, 1, t * P:(t + 1) * P],
                                         OT[:, h, (4 * g + t) * P:(4 * g + t + 1) * P], wo_s[:, h, :],
                                         start=(h == 0), stop=(h == QUAD - 1))
                done.then_inc(s_fill, 1)

            def pe_run(i, steps, first=False, last=False):
                for s in steps:
                    ahead, u, j = s["ahead"], s["unit"], s["j"]
                    transposes(i, ahead, u, j, first)
                    if last and (u, j) in TRANSPOSE_AT:
                        transpose_input(2, TRANSPOSE_AT[u, j])
                    for what in K_PE:
                        if what == "S":
                            for tile in s["score"]:
                                scores(i, tile)
                        if what == "F":
                            for f, k in s["fills"]:
                                project(i, ahead + 1, f, fill_no(i, k, first))
                            for g, k in s["outs"]:
                                project_out(i, g, fill_no(i, k))
                        if what == "V":
                            if j:
                                values(i, ahead, u, j - 1, first)
                            elif not first:
                                values(i, ahead - (u == 0), (u - 1) % UNITS, UNIT_STEPS - 1)

            for f in range(PROJ):
                project(0, 0, f, f, fixed=True)
            pe.wait_ge(s_bias_in, 16 * 4)
            for c in range(8):
                pe.matmul(OM[:, 1, 0:E], bv_col[:, c:c + 1].to_broadcast([P, P]), wo_half[c // 4][:, (c % 4) * E:(c % 4 + 1) * E],
                          start=(c == 0), stop=False)
            pe.matmul(OM[:, 1, 0:E], one_row, bo_row, start=False, stop=True).then_inc(s_bias_ps, 1)
            pe.wait_ge(s_misc, PROJ)
            for k in (3, 2, 1, 0):
                scores(0, (0, 0, k))
            scores(0, (0, 1, 3))
            pe_run(0, HEAD, first=True)
            with pe.Fori(0, ITERS - 1) as i:
                pe_run(i, BODY)
            pe_run(ITERS - 1, TAIL, last=True)
            values(ITERS - 1, 0, UNITS - 1, UNIT_STEPS - 1)
            project_out(ITERS - 1, 1, fill_no(ITERS - 1, 1))

            pe.wait_ge(s_zero, 4)
            pe.wait_ge(s_p2, ALL_STEPS * ITERS)
            keys_gates(1, 0)
            keys_gates(1, 1)
            ffn_values(1, 0)
            transpose_input(2, 2)
            transpose_input(2, 3)
            ffn_values(1, 1)
            keys_gates(1, 2)
            keys_gates(1, 3)
            ffn_values(1, 2)
            ffn_values(1, 3)


def rotary_tables():
    theta = np.float32(10000.0) ** (np.arange(0, DK, 2, dtype=np.float32) / np.float32(DK))
    freqs = np.arange(S, dtype=np.float32)[:, None] * (np.float32(1.0) / theta)[None, :]
    emb = np.concatenate([freqs, freqs], axis=-1).T
    even, odd = np.tile(emb[0::2], (QUAD, 1)), np.tile(emb[1::2], (QUAD, 1))
    return np.stack([np.cos(even), np.sin(odd), np.cos(odd), -np.sin(even)], axis=1).astype(np.float32)


def kernel(**inputs):
    import concourse.bacc as bacc
    from concourse.bass_utils import run_bass_kernel_spmd

    a = {k: np.asarray(v) for k, v in inputs.items()}

    def halves(w):
        w = w.reshape(QUADS, QUAD, HALF, 2, -1).transpose(0, 3, 1, 2, 4)
        return w.reshape(QUADS, 2, P, -1)

    qk = np.concatenate([halves(a["L0_attn_wq"]), halves(a["L0_attn_wk"])], axis=1)
    qk = qk.transpose(0, 3, 1, 2).reshape(QUADS, E, W_QK)
    wv = a["L0_attn_wv"].reshape(QUADS, W_V, E).transpose(0, 2, 1)
    biases = np.concatenate([halves(a["L0_attn_bq"]), halves(a["L0_attn_bk"])], axis=1)[..., 0]
    arrays = {
        "x": a["L0_attn_x"],
        "w_heads": np.concatenate([qk, wv], axis=2),
        "b_heads": biases.transpose(0, 2, 1),
        "wo_t": a["L0_attn_wo"].T,
        "bv": a["L0_attn_bv"].reshape(8, P).T,
        "bo": a["L0_attn_bo"].reshape(1, E),
        "rope": rotary_tables(),
        "wr_t": a["L0_ffn_W_r"].T,
        "wk_t": a["L0_ffn_W_k"].T,
        "wv_t": a["L0_ffn_W_v"].T,
        "mu": np.stack([a["L0_ffn_mu_r"], a["L0_ffn_mu_k"]], axis=1),
    }
    arrays = {k: np.ascontiguousarray(v) for k, v in arrays.items()}
    nc = bacc.Bacc("TRN2", target_bir_lowering=False, num_devices=1)
    aps = [nc.dram_tensor("in_" + k, v.shape, F32, kind="ExternalInput").ap() for k, v in arrays.items()]
    out = nc.dram_tensor("y", (B, S, E), F32, kind="ExternalOutput").ap()
    macaron(nc, *aps, out)
    result = run_bass_kernel_spmd(nc, [{"in_" + k: v for k, v in arrays.items()}], core_ids=[0])
    return result.results[0]["y"]
```
